# Optimizing a Trainium2 kernel written in Bass

```python
import numpy as np
import jax
import jax.numpy as jnp

def _softmax(x, axis=-1):
    return jax.nn.softmax(x, axis=axis)

def _gelu(x):
    return jax.nn.gelu(x, approximate=True)

def _silu(x):
    return jax.nn.silu(x)

def _sigmoid(x):
    return jax.nn.sigmoid(x)

def _layernorm(x, axis=-1, eps=1e-05):
    m = jnp.mean(x, axis=axis, keepdims=True)
    v = jnp.var(x, axis=axis, keepdims=True)
    return (x - m) / jnp.sqrt(v + eps)

def _scatter_add(tgt, idx, src, axis=0):
    return tgt.at[idx].add(src)

def _segment_sum(src, seg, n):
    return jax.ops.segment_sum(src, seg, n)
kernel_name = 'mk_gnn_preln_d1_gnn_r8_f4bf5b'

def setup_inputs(seed: int=0):
    np.random.seed(seed)
    _w = jnp.asarray

    def _rec_inputs():
        import jax
        import jax.numpy as jnp
        _gk = jax.random.key(seed)
        x = 8.953e-05 + 1 * jax.random.normal(jax.random.fold_in(_gk, 1), (12500, 16), jnp.float32)
        _s = jax.random.randint(jax.random.fold_in(_gk, 2), (200000,), 0, 12500, jnp.int32)
        _d = jax.random.randint(jax.random.fold_in(_gk, 3), (200000,), 0, 12500, jnp.int32)
        _loop = jnp.arange(12500, dtype=jnp.int32)
        src = jnp.concatenate([_s, _d, _loop])
        dst = jnp.concatenate([_d, _s, _loop])
        _o = jnp.argsort(dst, stable=True)
        src = src[_o]
        dst = dst[_o]
        edge_attr_3 = -1.09012e-05 + 0.99985 * jax.random.normal(jax.random.fold_in(_gk, 11), (412500, 3), jnp.float32)
        edge_attr_48 = -3.69585e-06 + 0.999911 * jax.random.normal(jax.random.fold_in(_gk, 12), (412500, 48), jnp.float32)
        return (x, src, dst, edge_attr_3, edge_attr_48)
    x, src, dst, edge_attr_3, edge_attr_48 = _rec_inputs()

    def _L0_gnn_setup():
        import jax, jax.numpy as jnp
        import numpy as np
        NS, NV = (16, 4)
        EPS = 1e-05
        N_NODES, N_EDGES = (5000, 50000)

        def _bn_scalar(x, g, b):
            m = x.mean(0)
            v = ((x - m) ** 2).mean(0)
            return (x - m) / jnp.sqrt(v + EPS) * g + b

        def _seg_mean(x, idx, n):
            s = jax.ops.segment_sum(x, idx, num_segments=n)
            c = jax.ops.segment_sum(jnp.ones((idx.shape[0],), x.dtype), idx, num_segments=n)
            return s / jnp.maximum(c, 1.0)[:, None]

        def _edge_weights(edge_attr, w1, b1, w2, b2):
            h = jax.nn.relu(edge_attr @ w1 + b1)
            return h @ w2 + b2

        def _forward(node_attr, edge_attr, edge_vec, fc0_w1, fc0_b1, fc0_w2, fc0_b2, fc1_w1, fc1_b1, fc1_w2, fc1_b2, bn0_gs, bn0_bs, bn0_gv, bn1_gs, bn1_bs, edge_index):
            N = node_attr.shape[0]
            E = edge_attr.shape[0]
            src, dst = (edge_index[0], edge_index[1])
            rhat = edge_vec / (jnp.linalg.norm(edge_vec, axis=-1, keepdims=True) + 1e-12)
            sh1 = rhat * float(np.sqrt(3.0))
            w = _edge_weights(edge_attr, fc0_w1, fc0_b1, fc0_w2, fc0_b2)
            wa = w[:, :NS * NS].reshape(E, NS, NS)
            wb = w[:, NS * NS:].reshape(E, NS, NV)
            x = node_attr[dst]
            inv = float(1.0 / np.sqrt(NS))
            msg_s = jnp.einsum('ei,eij->ej', x, wa) * inv
            msg_v = jnp.einsum('ei,eij,ec->ejc', x, wb, sh1) * inv
            msg = jnp.concatenate([msg_s, msg_v.reshape(E, NV * 3)], axis=-1)
            out = _seg_mean(msg, src, N)
            s0 = _bn_scalar(out[:, :NS], bn0_gs, bn0_bs)
            v0 = out[:, NS:].reshape(N, NV, 3)
            vn = jnp.sqrt((v0 ** 2).mean(axis=(0, 2)) + EPS)
            v0 = v0 / vn[None, :, None] * bn0_gv[None, :, None]
            w = _edge_weights(edge_attr, fc1_w1, fc1_b1, fc1_w2, fc1_b2)
            wa = w[:, :NS * NS].reshape(E, NS, NS)
            wb = w[:, NS * NS:].reshape(E, NV, NS)
            s = s0[dst]
            v = v0[dst]
            path_a = jnp.einsum('ei,eij->ej', s, wa)
            path_b = jnp.einsum('eic,ec,eij->ej', v, sh1, wb) * float(1.0 / np.sqrt(3.0))
            msg = (path_a + path_b) * float(1.0 / np.sqrt(NS + NV))
            node1 = _seg_mean(msg, src, N)
            return _bn_scalar(node1, bn1_gs, bn1_bs)
        key = jax.random.key(seed)
        ks = jax.random.split(key, 8)
        d = 3 * NS
        wn = NS * NS + NS * NV
        g = lambda k, shape, sc: jax.random.normal(k, shape, jnp.float32) * sc
        return {'node_attr': g(ks[0], (N_NODES, NS), 1.0), 'edge_attr': g(ks[1], (N_EDGES, d), 1.0), 'edge_vec': g(ks[2], (N_EDGES, 3), 1.0), 'fc0_w1': g(ks[3], (d, d), d ** (-0.5)), 'fc0_b1': jnp.zeros((d,), jnp.float32), 'fc0_w2': g(ks[4], (d, wn), d ** (-0.5)), 'fc0_b2': jnp.zeros((wn,), jnp.float32), 'fc1_w1': g(ks[5], (d, d), d ** (-0.5)), 'fc1_b1': jnp.zeros((d,), jnp.float32), 'fc1_w2': g(ks[6], (d, wn), d ** (-0.5)), 'fc1_b2': jnp.zeros((wn,), jnp.float32), 'bn0_gs': jnp.ones((NS,), jnp.float32), 'bn0_bs': jnp.zeros((NS,), jnp.float32), 'bn0_gv': jnp.ones((NV,), jnp.float32), 'bn1_gs': jnp.ones((NS,), jnp.float32), 'bn1_bs': jnp.zeros((NS,), jnp.float32), 'edge_index': jax.random.randint(ks[7], (2, N_EDGES), 0, N_NODES)}
    _L0_gnn_all = _L0_gnn_setup()
    _L0_gnn_in = {k: v for k, v in _L0_gnn_all.items() if k in ('fc0_w1', 'fc0_b1', 'fc0_w2', 'fc0_b2', 'fc1_w1', 'fc1_b1', 'fc1_w2', 'fc1_b2', 'bn0_gs', 'bn0_bs', 'bn0_gv', 'bn1_gs', 'bn1_bs')}
    del _L0_gnn_all
    return {'x': x, 'src': src, 'dst': dst, 'edge_attr_3': edge_attr_3, 'edge_attr_48': edge_attr_48, 'L0_gnn_fc0_w1': _L0_gnn_in['fc0_w1'], 'L0_gnn_fc0_b1': _L0_gnn_in['fc0_b1'], 'L0_gnn_fc0_w2': _L0_gnn_in['fc0_w2'], 'L0_gnn_fc0_b2': _L0_gnn_in['fc0_b2'], 'L0_gnn_fc1_w1': _L0_gnn_in['fc1_w1'], 'L0_gnn_fc1_b1': _L0_gnn_in['fc1_b1'], 'L0_gnn_fc1_w2': _L0_gnn_in['fc1_w2'], 'L0_gnn_fc1_b2': _L0_gnn_in['fc1_b2'], 'L0_gnn_bn0_gs': _L0_gnn_in['bn0_gs'], 'L0_gnn_bn0_bs': _L0_gnn_in['bn0_bs'], 'L0_gnn_bn0_gv': _L0_gnn_in['bn0_gv'], 'L0_gnn_bn1_gs': _L0_gnn_in['bn1_gs'], 'L0_gnn_bn1_bs': _L0_gnn_in['bn1_bs']}

def reference(x, src, dst, edge_attr_3, edge_attr_48, L0_gnn_fc0_w1, L0_gnn_fc0_b1, L0_gnn_fc0_w2, L0_gnn_fc0_b2, L0_gnn_fc1_w1, L0_gnn_fc1_b1, L0_gnn_fc1_w2, L0_gnn_fc1_b2, L0_gnn_bn0_gs, L0_gnn_bn0_bs, L0_gnn_bn0_gv, L0_gnn_bn1_gs, L0_gnn_bn1_bs):
    import jax
    import jax.numpy as jnp

    def _L0_gnn_ref(node_attr, edge_attr, edge_vec, fc0_w1, fc0_b1, fc0_w2, fc0_b2, fc1_w1, fc1_b1, fc1_w2, fc1_b2, bn0_gs, bn0_bs, bn0_gv, bn1_gs, bn1_bs, edge_index):
        import jax, jax.numpy as jnp
        import numpy as np
        NS, NV = (16, 4)
        EPS = 1e-05
        N_NODES, N_EDGES = (5000, 50000)

        def _bn_scalar(x, g, b):
            m = x.mean(0)
            v = ((x - m) ** 2).mean(0)
            return (x - m) / jnp.sqrt(v + EPS) * g + b

        def _seg_mean(x, idx, n):
            s = jax.ops.segment_sum(x, idx, num_segments=n)
            c = jax.ops.segment_sum(jnp.ones((idx.shape[0],), x.dtype), idx, num_segments=n)
            return s / jnp.maximum(c, 1.0)[:, None]

        def _edge_weights(edge_attr, w1, b1, w2, b2):
            h = jax.nn.relu(edge_attr @ w1 + b1)
            return h @ w2 + b2

        def _forward(node_attr, edge_attr, edge_vec, fc0_w1, fc0_b1, fc0_w2, fc0_b2, fc1_w1, fc1_b1, fc1_w2, fc1_b2, bn0_gs, bn0_bs, bn0_gv, bn1_gs, bn1_bs, edge_index):
            N = node_attr.shape[0]
            E = edge_attr.shape[0]
            src, dst = (edge_index[0], edge_index[1])
            rhat = edge_vec / (jnp.linalg.norm(edge_vec, axis=-1, keepdims=True) + 1e-12)
            sh1 = rhat * float(np.sqrt(3.0))
            w = _edge_weights(edge_attr, fc0_w1, fc0_b1, fc0_w2, fc0_b2)
            wa = w[:, :NS * NS].reshape(E, NS, NS)
            wb = w[:, NS * NS:].reshape(E, NS, NV)
            x = node_attr[dst]
            inv = float(1.0 / np.sqrt(NS))
            msg_s = jnp.einsum('ei,eij->ej', x, wa) * inv
            msg_v = jnp.einsum('ei,eij,ec->ejc', x, wb, sh1) * inv
            msg = jnp.concatenate([msg_s, msg_v.reshape(E, NV * 3)], axis=-1)
            out = _seg_mean(msg, src, N)
            s0 = _bn_scalar(out[:, :NS], bn0_gs, bn0_bs)
            v0 = out[:, NS:].reshape(N, NV, 3)
            vn = jnp.sqrt((v0 ** 2).mean(axis=(0, 2)) + EPS)
            v0 = v0 / vn[None, :, None] * bn0_gv[None, :, None]
            w = _edge_weights(edge_attr, fc1_w1, fc1_b1, fc1_w2, fc1_b2)
            wa = w[:, :NS * NS].reshape(E, NS, NS)
            wb = w[:, NS * NS:].reshape(E, NV, NS)
            s = s0[dst]
            v = v0[dst]
            path_a = jnp.einsum('ei,eij->ej', s, wa)
            path_b = jnp.einsum('eic,ec,eij->ej', v, sh1, wb) * float(1.0 / np.sqrt(3.0))
            msg = (path_a + path_b) * float(1.0 / np.sqrt(NS + NV))
            node1 = _seg_mean(msg, src, N)
            return _bn_scalar(node1, bn1_gs, bn1_bs)
        return _forward(node_attr, edge_attr, edge_vec, fc0_w1, fc0_b1, fc0_w2, fc0_b2, fc1_w1, fc1_b1, fc1_w2, fc1_b2, bn0_gs, bn0_bs, bn0_gv, bn1_gs, bn1_bs, edge_index)
    edge_index = jnp.stack([src, dst])
    h = jnp.maximum(_layernorm(x, axis=-1), 0.0)
    x = x + _L0_gnn_ref(h, edge_attr_48, edge_attr_3, L0_gnn_fc0_w1, L0_gnn_fc0_b1, L0_gnn_fc0_w2, L0_gnn_fc0_b2, L0_gnn_fc1_w1, L0_gnn_fc1_b1, L0_gnn_fc1_w2, L0_gnn_fc1_b2, L0_gnn_bn0_gs, L0_gnn_bn0_bs, L0_gnn_bn0_gv, L0_gnn_bn1_gs, L0_gnn_bn1_bs, edge_index)
    return x

_drawn_inputs = setup_inputs


def setup_inputs(seed=0):
    import zlib

    import numpy as np

    out = dict(_drawn_inputs(seed))
    spreads = {'L0_gnn_fc0_b1': (0.0, 0.1),
     'L0_gnn_fc0_b2': (0.0, 0.1),
     'L0_gnn_fc1_b1': (0.0, 0.1),
     'L0_gnn_fc1_b2': (0.0, 0.1),
     'L0_gnn_bn0_gs': (1.0, 0.2),
     'L0_gnn_bn0_bs': (0.0, 0.1),
     'L0_gnn_bn0_gv': (1.0, 0.2),
     'L0_gnn_bn1_gs': (1.0, 0.2),
     'L0_gnn_bn1_bs': (0.0, 0.1)}
    factors = {}
    for name, (base, spread) in spreads.items():
        noise = np.random.default_rng([zlib.crc32(name.encode()), seed]).standard_normal(out[name].shape)
        drawn = base * np.exp(spread * noise) if base else spread * noise
        out[name] = jnp.asarray(drawn.astype(out[name].dtype))
    for name, factor in factors.items():
        out[name] = (out[name] * factor).astype(out[name].dtype)
    return out
```

```python
from contextlib import ExitStack

import numpy as np

import concourse.bass as bass
from concourse import mybir

F32 = mybir.dt.float32
BF16 = mybir.dt.bfloat16
I32 = mybir.dt.int32
U32 = mybir.dt.uint32
ALU = mybir.AluOpType
ACT = mybir.ActivationFunctionType
AX_X = mybir.AxisListType.X

P = 128
N = 12500
E = 412500
NS, NV, XYZ = 16, 4, 3
D = 3 * NS
HK = D + 1
WN = NS * NS + NS * NV
EPS = 1e-5
TILES = 8
STEP = TILES * P
HALF = STEP // 2
STEPS = -(-E // STEP)
ALL_TILES = STEPS * TILES
EP = STEPS * STEP
PAD_NODE = N
TABLES = TILES
TABLE_ROWS = 12672
FIRST_SPARE = N + 1
NODE_PARTS, NODE_COLS = 125, 100
ROW = 32
PAIRS = TILES // 2
GROUP = 4
assert STEPS % 2 == 1 and NODE_PARTS * NODE_COLS == N and TABLE_ROWS >= FIRST_SPARE + P

T0, S0, V0, ONE, COLS1 = 1, 5, 21, 33, 34
ROW_S, ROW_V, ROW_ONE = S0 - 2, V0 - 2, ONE - 2
NODE_V, NODE_U, NODE_S = 0, 12, 16
COLS2 = NS


def after(eng, sem, value):
    if not isinstance(value, int) or value > 0:
        eng.wait_ge(sem, value)


def prepare(nc, a, dram, keep):
    with ExitStack() as ctx:
        def sb(name, shape, dt):
            return ctx.enter_context(nc.sbuf_tensor(name, shape, dt))

        def sem(name):
            return ctx.enter_context(nc.semaphore(name))

        zero = sb("zero", [P, TABLE_ROWS * ROW // P], F32)
        recv_i = sb("recv_i", [P, ALL_TILES], I32)
        part_i = sb("part_i", [P, ALL_TILES], I32)
        high = sb("high", [P, ALL_TILES], BF16)
        low = sb("low", [P, ALL_TILES], BF16)
        norm2 = sb("norm2", [P, ALL_TILES], F32)
        length = sb("length", [P, ALL_TILES], F32)
        CH = ALL_TILES // 13
        square = sb("square", [P, CH, XYZ], F32)
        xn = sb("xn", [NODE_PARTS, NODE_COLS, NS], F32)
        xc = sb("xc", [NODE_PARTS, NODE_COLS, NS], F32)
        xq = sb("xq", [NODE_PARTS, NODE_COLS, NS], F32)
        mean = sb("mean", [NODE_PARTS, NODE_COLS], F32)
        var = sb("var", [NODE_PARTS, NODE_COLS], F32)
        std = sb("std", [NODE_PARTS, NODE_COLS], F32)
        rstd = sb("rstd", [NODE_PARTS, NODE_COLS], F32)

        x_in, vec_in, recv_in, row_in = sem("x_in"), sem("vec_in"), sem("recv_in"), sem("row_in")
        const_in, zeroed, tables_out = sem("const_in"), sem("zeroed"), sem("tables_out")
        dve_step, split, rows_out = sem("dve_step"), sem("split"), sem("rows_out")
        var_done, std_done, x_done, x_out = sem("var_done"), sem("std_done"), sem("x_done"), sem("x_out")
        norm_done, length_done = sem("norm_done"), sem("length_done")

        with nc.Block() as block:
            @block.sync
            def _(sp):
                sp.dma_start(xn[:], a["x"].rearrange("(p c) k -> p c k", p=NODE_PARTS)).then_inc(x_in, 16)
                sp.dma_start(recv_i[:], a["recv_flat"]).then_inc(row_in, 16)
                sp.dma_start(keep["unit"][:], a["vec"]).then_inc(vec_in, 16)
                sp.dma_start(keep["sender"][:], a["send_cols"]).then_inc(const_in, 16)
                for k in (1, 2):
                    for h in (0, 64):
                        sp.dma_start(keep[f"w1_{k}"][h:h + D, 0:D], a[f"w1_{k}"]).then_inc(const_in, 16)
                        sp.dma_start(keep[f"b1_{k}"][h:h + D, :], a[f"b1_{k}"]).then_inc(const_in, 16)
                        sp.dma_start(keep[f"w2_{k}"][h:h + D, :], a[f"w2_{k}"]).then_inc(const_in, 16)
                        sp.dma_start(keep[f"w2_{k}"][h + D:h + HK, :], a[f"b2_{k}"]).then_inc(const_in, 16)
                sp.dma_start(keep["by_part"][:], a["by_part"]).then_inc(const_in, 16)
                sp.wait_ge(split, 1)
                sp.dma_start(dram["recv_rows"][0].rearrange("(p t) -> p t", p=P), high[:]).then_inc(rows_out, 16)
                sp.dma_start(dram["recv_rows"][1].rearrange("(p t) -> p t", p=P), low[:]).then_inc(rows_out, 16)
                sp.dma_start(recv_i[:], a["recv_cols"]).then_inc(recv_in, 16)
                sp.wait_ge(zeroed, 1)
                for j in range(TABLES):
                    sp.dma_start(dram["sum1"][j].rearrange("(p r) k -> p (r k)", p=P), zero[:]).then_inc(tables_out, 16)
                    sp.dma_start(dram["sum2"][j].rearrange("(p r) k -> p (r k)", p=P),
                                 zero[:, 0:TABLE_ROWS * COLS2 // P]).then_inc(tables_out, 16)
                sp.wait_ge(x_done, 1)
                sp.dma_start(dram["norm_x"].rearrange("(p c) k -> p c k", p=NODE_PARTS), xc[:]).then_inc(x_out, 16)
                sp.wait_ge(x_out, 16)
                sp.wait_ge(rows_out, 32)
                sp.wait_ge(tables_out, 2 * 16 * TABLES)
                sp.wait_ge(const_in, 18 * 16)

            @block.gpsimd
            def _(pool):
                nc.gpsimd.memset(zero[:], 0.0).then_inc(zeroed, 1)

            @block.scalar
            def _(act):
                act.wait_ge(var_done, 1)
                nc.scalar.activation(std[:], var[:], ACT.Sqrt).then_inc(std_done, 1)
                act.wait_ge(norm_done, 13)
                nc.scalar.activation(length[:], norm2[:], ACT.Sqrt).then_inc(length_done, 1)

            @block.vector
            def _(dve):
                steps = [0]

                def then(ins):
                    steps[0] += 1
                    ins.then_inc(dve_step, 1)
                    dve.wait_ge(dve_step, steps[0])

                per_node = [NODE_PARTS, NODE_COLS, NS]
                dve.wait_ge(x_in, 16)
                then(nc.vector.reduce_sum(mean[:], xn[:], AX_X))
                then(nc.vector.tensor_scalar(mean[:], mean[:], 1.0 / NS, None, ALU.mult))
                then(nc.vector.tensor_tensor(xc[:], xn[:], mean[:].unsqueeze(2).to_broadcast(per_node), ALU.subtract))
                then(nc.vector.tensor_tensor(xq[:], xc[:], xc[:], ALU.mult))
                then(nc.vector.reduce_sum(var[:], xq[:], AX_X))
                nc.vector.tensor_scalar(var[:], var[:], 1.0 / NS, EPS, ALU.mult, ALU.add).then_inc(var_done, 1)

                dve.wait_ge(row_in, 16)
                then(nc.vector.tensor_scalar(part_i[:], recv_i[:], 7, None, ALU.logical_shift_right))
                then(nc.vector.tensor_copy(high[:], part_i[:]))
                then(nc.vector.tensor_scalar(part_i[:], recv_i[:], 127, None, ALU.bitwise_and))
                nc.vector.tensor_copy(low[:], part_i[:]).then_inc(split, 1)

                dve.wait_ge(std_done, 1)
                then(nc.vector.reciprocal(rstd[:], std[:]))
                then(nc.vector.tensor_tensor(xc[:], xc[:], rstd[:].unsqueeze(2).to_broadcast(per_node), ALU.mult))
                nc.vector.tensor_scalar(xc[:], xc[:], 0.0, None, ALU.max).then_inc(x_done, 1)

                dve.wait_ge(const_in, 18 * 16)
                then(nc.vector.tensor_copy(keep["combine1"][:, :, :, 0],
                                           keep["by_part"][:, 0:1].unsqueeze(2).to_broadcast([P, 2, TILES])))

                unit = keep["unit"]
                dve.wait_ge(vec_in, 16)
                for c in range(13):
                    then(nc.vector.tensor_tensor(square[:], unit[:, c * CH:(c + 1) * CH, :],
                                                 unit[:, c * CH:(c + 1) * CH, :], ALU.mult))
                    nc.vector.reduce_sum(norm2[:, c * CH:(c + 1) * CH], square[:], AX_X).then_inc(norm_done, 1)
                    dve.wait_ge(norm_done, c + 1)
                dve.wait_ge(length_done, 1)
                then(nc.vector.tensor_scalar(length[:], length[:], 1e-12, None, ALU.add))
                then(nc.vector.reciprocal(norm2[:], length[:]))
                then(nc.vector.scalar_tensor_tensor(
                    out=unit[:], in0=unit[:], scalar=float(np.sqrt(3.0)),
                    in1=norm2[:].unsqueeze(2).to_broadcast([P, ALL_TILES, XYZ]), op0=ALU.mult, op1=ALU.mult))

                dve.wait_ge(recv_in, 16)
                then(nc.vector.tensor_copy(keep["recv"][:], recv_i[:]))


def constants(nc, keep):
    filled = nc.semaphore("filled")
    with filled as filled, nc.Block() as block:
        @block.vector
        def _(dve):
            n = 0
            for k in (1, 2):
                nc.vector.memset(keep[f"w1_{k}"][:], 0.0).then_inc(filled, 1)
                nc.vector.memset(keep[f"b1_{k}"][:], 1.0).then_inc(filled, 1)
            nc.vector.memset(keep["combine1"][:], 1.0).then_inc(filled, 1)
            nc.vector.memset(keep["halves"][:], 1.0).then_inc(filled, 1)
            dve.wait_ge(filled, 6)
            nc.vector.memset(keep["halves"][0:1, :], float(P)).then_inc(filled, 1)
            dve.wait_ge(filled, 7)


def edge_layer(nc, a, dram, keep, layer):
    first = layer == 1
    COLS = COLS1 if first else COLS2
    IN, OUT = (NS, NV + NS) if first else (NV + NS, NS)
    table = dram["norm_x"] if first else dram["node"]
    GW = NS if first else ROW
    sums = dram["sum1"] if first else dram["sum2"]
    SW = ROW if first else COLS2
    w1, b1, w2 = (keep[f"{n}_{layer}"] for n in ("w1", "b1", "w2"))
    unit, recv, sender, target = keep["unit"], keep["recv"], keep["sender"], keep["target"]

    with ExitStack() as ctx:
        def sb(name, shape, dt):
            return ctx.enter_context(nc.sbuf_tensor(f"{name}_{layer}", shape, dt))

        def pb(name):
            return ctx.enter_context(nc.psum_tensor(f"{name}_{layer}", [P, 512], F32))

        def sem(name):
            return ctx.enter_context(nc.semaphore(f"{name}_{layer}"))

        def two(name):
            return [sem(f"{name}_even"), sem(f"{name}_odd")]

        attr = sb("attr", [P, 2, HALF], F32)
        recv_row = sb("recv_row", [2, 2, STEP], BF16)
        hidden = sb("hidden", [P, 2, HALF], F32)
        send_idx = sb("send_idx", [P, 2, TILES], U32)
        target_idx = sb("target_idx", [P, 2, TILES], U32)
        node = sb("node", [P, 2, TILES, GW], F32)
        prod = sb("prod", [P, 2, 2, WN], F32)
        same = sb("same", [P, 2, TILES, P], F32)
        rows = sb("rows", [P, 2, TILES, COLS], F32)
        combine = keep["combine1"] if first else sb("combine", [P, 2, TILES, COLS], F32)
        vdot = sb("vdot", [P, TILES, NV, XYZ], F32)
        shift = sb("shift", [P, TILES], F32)

        hid_ps = [pb("hid_a"), pb("hid_b")]
        weight_ps = ctx.enter_context(nc.psum_tensor(f"weight_ps_{layer}", [P, 2, 2, 512], F32))
        recv_ps = pb("recv_ps")
        comb_ps = pb("comb_ps")
        comb = comb_ps[:, 0:TILES * COLS].rearrange("p (t k) -> p t k", k=COLS)

        gate = sem("gate")
        loaded = two("loaded")
        gathered = two("gathered")
        scattered = [sem(f"scattered{j}") for j in range(TABLES)]
        rows_free = sem("rows_free")
        send_staged = sem("send_staged")
        hid_done = sem("hid_done")
        hidden_ready = sem("hidden_ready")
        weights_ready = sem("weights_ready")
        weights_used = sem("weights_used")
        reduced = sem("reduced")
        recv_ready = sem("recv_ready")
        same_done = sem("same_done")
        vectors_done = sem("vectors_done")
        comb_done = sem("comb_done")
        rows_ready = sem("rows_ready")
        shift_done = sem("shift_done")
        target_done = sem("target_done")
        target_staged = sem("target_staged")

        class Step:

            def __init__(self, half, odd):
                self.half, self.odd = half, odd
                self.n = half * 2 + odd

            def next(self):
                return Step(self.half, 1) if self.odd == 0 else Step(self.half + 1, 0)

            def prev(self):
                return Step(self.half, 0) if self.odd == 1 else Step(self.half - 1, 1)

            @property
            def has_prev(self):
                return not isinstance(self.n, int) or self.n > 0

            @property
            def has_next(self):
                return not isinstance(self.n, int) or self.n < STEPS - 1

            def cols(self, of, start=0, width=TILES):
                return of[:, bass.ds(self.n * TILES + start, width)]

        def every_step(eng, body):
            for n in range(3):
                body(Step(n // 2, n % 2))
            with eng.Fori(1, STEPS // 2 - 1) as half:
                body(Step(half, 1))
                body(Step(half + 1, 0))
            for n in (STEPS - 2, STEPS - 1):
                body(Step(n // 2, n % 2))

        with nc.Block() as block:
            @block.sync
            def _(sp):
                def load(s):
                    after(sp, recv_ready, (s.n - 1) * (TILES // GROUP))
                    sp.sem_inc(gate, 1)
                    for h in range(2):
                        sp.dma_start(attr[64 * h:64 * h + D, s.odd, :],
                                     a["attr"][h][:, bass.ds(s.n * HALF, HALF)]).then_inc(loaded[s.odd], 16)
                    sp.dma_start(recv_row[:, s.odd, :],
                                 dram["recv_rows"][:, bass.ds(s.n * STEP, STEP)]).then_inc(loaded[s.odd], 16)

                every_step(sp, load)

            @block.gpsimd
            def _(pool):
                def gather(s):
                    after(pool, send_staged, s.n + 1)
                    after(pool, weights_used, PAIRS * (s.n - 1))
                    pool.sem_inc(gate, 1)
                    for j in range(TILES):
                        nc.gpsimd.indirect_dma_start(
                            node[:, s.odd, j, :], None, table[:, :],
                            bass.IndirectOffsetOnAxis(send_idx[:, s.odd, j:j + 1], 0),
                        ).then_inc(gathered[s.odd], 16)

                def scatter(s):
                    after(pool, rows_ready, s.n + 1)
                    after(pool, target_staged, s.n + 1)
                    for j in range(TABLES):
                        after(pool, scattered[j], s.n * 16)
                    pool.sem_inc(rows_free, 1)
                    for j in range(TABLES):
                        nc.gpsimd.indirect_dma_start(
                            sums[j][:, :], bass.IndirectOffsetOnAxis(target_idx[:, s.odd, j:j + 1], 0),
                            rows[:, s.odd, j, COLS - SW:COLS], None, compute_op=ALU.add,
                        ).then_inc(scattered[j], 16)

                def body(s):
                    if s.has_next:
                        gather(s.next())
                    if s.has_prev:
                        scatter(s.prev())

                gather(Step(0, 0))
                every_step(pool, body)
                scatter(Step(STEPS // 2, 0))
                for j in range(TABLES):
                    pool.wait_ge(scattered[j], STEPS * 16)

            @block.scalar
            def _(act):
                def stage_sender(s):
                    after(act, gathered[s.odd], s.half * TILES * 16)
                    nc.scalar.copy(send_idx[:, s.odd, :], s.cols(sender)).then_inc(send_staged, 1)

                def relu(s):
                    after(act, hid_done, s.n + 1)
                    after(act, weights_ready, PAIRS * (s.n - 1))
                    for h in range(2):
                        rng = slice(64 * h, 64 * h + HK)
                        nc.scalar.activation(hidden[rng, s.odd, :], hid_ps[h][rng, :], ACT.Relu,
                                             bias=b1[rng, :]).then_inc(hidden_ready, 1)

                def move_rows(s):
                    after(act, rows_free, s.n)
                    after(act, comb_done, s.n + 1)
                    nc.scalar.copy(rows[:, s.odd, :, :], comb).then_inc(rows_ready, 1)
                    if first:
                        after(act, target_done, s.n + 1)
                    nc.scalar.copy(target_idx[:, s.odd, :], s.cols(target)).then_inc(target_staged, 1)

                def body(s):
                    if s.has_next:
                        stage_sender(s.next())
                        relu(s.next())
                    if s.has_prev:
                        move_rows(s.prev())

                stage_sender(Step(0, 0))
                relu(Step(0, 0))
                every_step(act, body)
                move_rows(Step(STEPS // 2, 0))

            @block.tensor
            def _(pe):
                def hidden_product(s):
                    after(pe, loaded[s.odd], (s.half + 1) * 3 * 16)
                    after(pe, hidden_ready, 2 * s.n)
                    pe.sem_inc(gate, 1)
                    for h in range(2):
                        lo = 64 * h
                        mm = nc.tensor.matmul(hid_ps[h][lo:lo + HK, :], w1[lo:lo + D, :],
                                              attr[lo:lo + D, s.odd, :], start=True, stop=True)
                    mm.then_inc(hid_done, 1)

                def weight_product(s, j):
                    after(pe, hidden_ready, 2 * s.n + 2)
                    after(pe, weights_used, PAIRS * s.n + j - 1)
                    for h in range(2):
                        lo = 64 * h
                        mm = nc.tensor.matmul(weight_ps[:, j % 2, h, 0:WN],
                                              hidden[lo:lo + HK, s.odd, j * P:(j + 1) * P],
                                              w2[lo:lo + HK, :], start=True, stop=True)
                    mm.then_inc(weights_ready, 1)

                def receivers(s, c):
                    after(pe, loaded[s.odd], (s.half + 1) * 3 * 16)
                    after(pe, same_done, 2 * s.n + c)
                    nc.tensor.matmul(recv_ps[:, :], keep["halves"][:, :],
                                     recv_row[:, s.odd, c * GROUP * P:(c + 1) * GROUP * P],
                                     start=True, stop=True).then_inc(recv_ready, 1)

                def combine_messages(s):
                    after(pe, same_done, 2 * s.n + 2)
                    if first:
                        after(pe, vectors_done, s.n + 1)
                    else:
                        after(pe, reduced, PAIRS * (s.n + 1))
                    after(pe, rows_ready, s.n)
                    for t in range(TILES):
                        mm = nc.tensor.matmul(comb[:, t, :], same[:, s.odd, t, :], combine[:, s.odd, t, :],
                                              start=True, stop=True)
                    mm.then_inc(comb_done, 1)

                def body(s):
                    if s.has_next:
                        hidden_product(s.next())
                    weight_product(s, 0)
                    weight_product(s, 1)
                    if s.has_prev:
                        combine_messages(s.prev())
                    receivers(s, 0)
                    weight_product(s, 2)
                    weight_product(s, 3)
                    receivers(s, 1)

                hidden_product(Step(0, 0))
                every_step(pe, body)
                combine_messages(Step(STEPS // 2, 0))

            @block.vector
            def _(dve):
                def vector_inputs(s):
                    if s.has_prev:
                        dve.wait_ge(vectors_done, s.n * 2)
                    nc.vector.tensor_tensor(
                        vdot[:], node[:, s.odd, :, NODE_V:NODE_V + NV * XYZ].rearrange("p t (j c) -> p t j c", c=XYZ),
                        s.cols(unit).unsqueeze(2).to_broadcast([P, TILES, NV, XYZ]),
                        ALU.mult).then_inc(vectors_done, 1)
                    dve.wait_ge(vectors_done, s.n * 2 + 1)
                    nc.vector.reduce_sum(node[:, s.odd, :, NODE_U:NODE_U + NV], vdot[:], AX_X).then_inc(vectors_done, 1)
                    dve.wait_ge(vectors_done, s.n * 2 + 2)

                def product(s, j):
                    dve.wait_ge(weights_ready, PAIRS * s.n + j + 1)
                    after(dve, reduced, PAIRS * s.n + j - 1)
                    w = weight_ps[:, j % 2, :, 0:WN].rearrange("p h (i o) -> p h i o", o=OUT)
                    x = node[:, s.odd, :, GW - IN:GW].rearrange("p (h j) i -> p h j i", h=2)[:, :, j, :]
                    nc.vector.tensor_tensor(
                        prod[:, j % 2, :, :].rearrange("p h (i o) -> p h i o", o=OUT), w,
                        x.unsqueeze(3).to_broadcast([P, 2, IN, OUT]), ALU.mult).then_inc(weights_used, 1)

                def reduce(s, j):
                    dve.wait_ge(weights_used, PAIRS * s.n + j + 1)
                    lo = T0 if first else 0
                    out = combine[:, s.odd, :, lo:lo + OUT].rearrange("p (h j) o -> p h j o", h=2)[:, :, j, :]
                    nc.vector.reduce_sum(out, prod[:, j % 2, :, :].rearrange("p h (i o) -> p h o i", o=OUT),
                                         AX_X).then_inc(reduced, 1)

                def equal_receivers(s, c):
                    dve.wait_ge(recv_ready, 2 * s.n + c + 1)
                    nc.vector.tensor_tensor(
                        same[:, s.odd, c * GROUP:(c + 1) * GROUP, :],
                        recv_ps[:, :].rearrange("p (t e) -> p t e", t=GROUP),
                        s.cols(recv, c * GROUP, GROUP).unsqueeze(2).to_broadcast([P, GROUP, P]),
                        ALU.is_equal).then_inc(same_done, 1)

                def vector_messages(s):
                    dve.wait_ge(reduced, PAIRS * (s.n + 1))
                    nc.vector.tensor_tensor(
                        combine[:, s.odd, :, V0:V0 + NV * XYZ].rearrange("p t (j c) -> p t j c", c=XYZ),
                        combine[:, s.odd, :, T0:T0 + NV].unsqueeze(3).to_broadcast([P, TILES, NV, XYZ]),
                        s.cols(unit).unsqueeze(2).to_broadcast([P, TILES, NV, XYZ]),
                        ALU.mult).then_inc(vectors_done, 1)

                def targets(s):
                    by_part = keep["by_part"]
                    dve.wait_ge(rows_ready, s.n + 1)
                    nc.vector.tensor_scalar(shift[:], s.cols(recv), -1.0, by_part[:, 2:3],
                                            ALU.mult, ALU.add).then_inc(shift_done, 1)
                    dve.wait_ge(shift_done, 2 * s.n + 1)
                    nc.vector.scalar_tensor_tensor(out=shift[:], in0=rows[:, s.odd, :, 0], scalar=by_part[:, 1:2],
                                                   in1=shift[:], op0=ALU.is_gt, op1=ALU.mult).then_inc(shift_done, 1)
                    dve.wait_ge(shift_done, 2 * s.n + 2)
                    nc.vector.tensor_tensor(s.cols(target), s.cols(recv), shift[:], ALU.add).then_inc(target_done, 1)

                def body(s):
                    dve.wait_ge(gathered[s.odd], (s.half + 1) * TILES * 16)
                    after(dve, comb_done, s.n - 1)
                    if not first:
                        vector_inputs(s)
                    product(s, 0)
                    product(s, 1)
                    reduce(s, 0)
                    product(s, 2)
                    reduce(s, 1)
                    equal_receivers(s, 0)
                    product(s, 3)
                    reduce(s, 2)
                    if first and s.has_prev:
                        targets(s.prev())
                    equal_receivers(s, 1)
                    reduce(s, 3)
                    if first:
                        vector_messages(s)

                every_step(dve, body)
                if first:
                    targets(Step(STEPS // 2, 0))


def node_layer(nc, a, dram, keep, layer, out):
    first = layer == 1
    sums, W = (dram["sum1"], ROW) if first else (dram["sum2"], COLS2)
    SCALE = 1.0 / np.sqrt(NS) if first else 1.0 / np.sqrt(NS + NV)
    S_AT = ROW_S if first else 0
    BUFS = 3
    PN, CN = NODE_PARTS, NODE_COLS
    with ExitStack() as ctx:
        def sb(name, shape):
            return ctx.enter_context(nc.sbuf_tensor(f"{name}_n{layer}", shape, F32))

        def sem(name):
            return ctx.enter_context(nc.semaphore(f"{name}_n{layer}"))

        total = sb("total", [PN, CN, W])
        part = sb("part", [PN, BUFS, CN * W])
        square = sb("square", [PN, CN, NS])
        ones = sb("ones", [PN, P])
        gain, bias = sb("gain", [PN, NS]), sb("bias", [PN, NS])
        vgain = sb("vgain", [PN, NV])
        colsum = sb("colsum", [PN, NS])
        mean = sb("mean", [PN, NS])
        var = sb("var", [PN, NS])
        std = sb("std", [PN, NS])
        result = sb("result", [PN, CN, ROW if first else NS])
        x_old = sb("x_old", [PN, CN, NS])
        stat_ps = ctx.enter_context(nc.psum_tensor(f"stat_ps_n{layer}", [P, 512], F32))
        table_in = [sem(f"table_in{b}") for b in range(BUFS)]
        total_in, par_in, ones_done, x_in = sem("total_in"), sem("par_in"), sem("ones_done"), sem("x_in")
        added, step, colsum_done, stat_done = sem("added"), sem("step"), sem("colsum_done"), sem("stat_done")
        var_done, std_done, result_done, result_out = (
            sem("var_done"), sem("std_done"), sem("result_done"), sem("result_out"))
        STATS = 3 if first else 2

        with nc.Block() as block:
            @block.sync
            def _(sp):
                def table_of(j):
                    return sums[j][0:N, :].rearrange("(p c) k -> p (c k)", p=PN)

                def row_of(v, n):
                    return v.rearrange("(o k) -> o k", o=1).to_broadcast([PN, n])

                sp.dma_start(total[:].rearrange("p c k -> p (c k)"), table_of(0)).then_inc(total_in, 16)
                for j in range(1, TABLES):
                    after(sp, added, j - BUFS)
                    sp.dma_start(part[:, j % BUFS, :], table_of(j)).then_inc(table_in[j % BUFS], 16)
                sp.dma_start(gain[:], row_of(a[f"gs_{layer}"], NS)).then_inc(par_in, 16)
                sp.dma_start(bias[:], row_of(a[f"bs_{layer}"], NS)).then_inc(par_in, 16)
                if first:
                    sp.dma_start(vgain[:], row_of(a["gv_1"], NV)).then_inc(par_in, 16)
                else:
                    sp.dma_start(x_old[:], a["x"].rearrange("(p c) k -> p c k", p=PN)).then_inc(x_in, 16)
                sp.wait_ge(result_done, 1)
                sp.dma_start(out.rearrange("(p c) k -> p c k", p=PN), result[:]).then_inc(result_out, 16)
                sp.wait_ge(result_out, 16)

            @block.gpsimd
            def _(pool):
                nc.gpsimd.memset(ones[:], 1.0).then_inc(ones_done, 1)

            @block.tensor
            def _(pe):
                pe.wait_ge(ones_done, 1)
                for n in range(STATS):
                    k = NS if n < 2 else NV
                    pe.wait_ge(colsum_done, n + 1)
                    nc.tensor.matmul(stat_ps[0:PN, n * NS:n * NS + k], ones[:, 0:PN], colsum[:, 0:k],
                                     start=True, stop=True).then_inc(stat_done, 1)

            @block.scalar
            def _(act):
                for n in range(STATS - 1):
                    k = NS if n < 1 else NV
                    act.wait_ge(var_done, n + 1)
                    nc.scalar.activation(std[:, 0:k], var[:, 0:k], ACT.Sqrt).then_inc(std_done, 1)

            @block.vector
            def _(dve):
                steps = [0]

                def then(ins):
                    steps[0] += 1
                    ins.then_inc(step, 1)
                    dve.wait_ge(step, steps[0])

                def over_nodes(v, k):
                    return v[:, 0:k].unsqueeze(1).to_broadcast([PN, CN, k])

                flat = total[:].rearrange("p c k -> p (c k)")
                dve.wait_ge(total_in, 16)
                for j in range(1, TABLES):
                    dve.wait_ge(table_in[j % BUFS], 16 * ((j - (j % BUFS or BUFS)) // BUFS + 1))
                    nc.vector.tensor_tensor(flat, flat, part[:, j % BUFS, :], ALU.add).then_inc(added, 1)
                    dve.wait_ge(added, j)
                per_count = keep["per_count"]
                if first:
                    then(nc.vector.tensor_scalar(per_count[:], total[:, :, ROW_ONE], 1.0, None, ALU.max))
                    then(nc.vector.reciprocal(per_count[:], per_count[:]))
                then(nc.vector.scalar_tensor_tensor(
                    out=total[:], in0=total[:], scalar=float(SCALE),
                    in1=per_count[:].unsqueeze(2).to_broadcast([PN, CN, W]), op0=ALU.mult, op1=ALU.mult))
                s = total[:, :, S_AT:S_AT + NS]
                nc.vector.reduce_sum(colsum[:], s.rearrange("p c k -> p k c"), AX_X).then_inc(colsum_done, 1)
                dve.wait_ge(stat_done, 1)
                then(nc.vector.tensor_scalar(mean[:], stat_ps[0:PN, 0:NS], 1.0 / N, None, ALU.mult))
                then(nc.vector.tensor_tensor(s, s, over_nodes(mean, NS), ALU.subtract))
                then(nc.vector.tensor_tensor(square[:], s, s, ALU.mult))
                nc.vector.reduce_sum(colsum[:], square[:].rearrange("p c k -> p k c"), AX_X).then_inc(colsum_done, 1)
                dve.wait_ge(stat_done, 2)
                nc.vector.tensor_scalar(var[:], stat_ps[0:PN, NS:2 * NS], 1.0 / N, EPS,
                                        ALU.mult, ALU.add).then_inc(var_done, 1)
                dve.wait_ge(std_done, 1)
                dve.wait_ge(par_in, 48 if first else 32)
                then(nc.vector.reciprocal(mean[:], std[:]))
                then(nc.vector.tensor_tensor(gain[:], gain[:], mean[:], ALU.mult))
                then(nc.vector.tensor_tensor(s, s, over_nodes(gain, NS), ALU.mult))
                if not first:
                    dve.wait_ge(x_in, 16)
                    then(nc.vector.tensor_tensor(s, s, over_nodes(bias, NS), ALU.add))
                    nc.vector.tensor_tensor(result[:], x_old[:], s, ALU.add).then_inc(result_done, 1)
                    return
                then(nc.vector.memset(result[:, :, NODE_U:NODE_S], 0.0))
                then(nc.vector.tensor_tensor(result[:, :, NODE_S:ROW], s, over_nodes(bias, NS), ALU.add))
                v = total[:, :, ROW_V:ROW_V + NV * XYZ]
                then(nc.vector.tensor_tensor(square[:, :, 0:NV * XYZ], v, v, ALU.mult))
                vsum = colsum[:, NV:NV + NV * XYZ]
                then(nc.vector.reduce_sum(vsum, square[:, :, 0:NV * XYZ].rearrange("p c k -> p k c"), AX_X))
                nc.vector.reduce_sum(colsum[:, 0:NV], vsum.rearrange("p (j c) -> p j c", c=XYZ),
                                     AX_X).then_inc(colsum_done, 1)
                dve.wait_ge(stat_done, 3)
                nc.vector.tensor_scalar(var[:, 0:NV], stat_ps[0:PN, 2 * NS:2 * NS + NV], 1.0 / (XYZ * N), EPS,
                                        ALU.mult, ALU.add).then_inc(var_done, 1)
                dve.wait_ge(std_done, 2)
                then(nc.vector.reciprocal(mean[:, 0:NV], std[:, 0:NV]))
                then(nc.vector.scalar_tensor_tensor(out=vgain[:], in0=vgain[:], scalar=float(1.0 / np.sqrt(3.0)),
                                                    in1=mean[:, 0:NV], op0=ALU.mult, op1=ALU.mult))
                then(nc.vector.tensor_copy(mean[:, 0:NV * XYZ].rearrange("p (j c) -> p j c", c=XYZ),
                                           vgain[:].unsqueeze(2).to_broadcast([PN, NV, XYZ])))
                nc.vector.tensor_tensor(result[:, :, NODE_V:NODE_V + NV * XYZ], v, over_nodes(mean, NV * XYZ),
                                        ALU.mult).then_inc(result_done, 1)


def gnn_kernel(nc, a, out):
    dram = {
        "norm_x": nc.dram_tensor("norm_x", [N, NS], F32),
        "node": nc.dram_tensor("node", [N, ROW], F32),
        "recv_rows": nc.dram_tensor("recv_rows", [2, EP], BF16),
        "sum1": [nc.dram_tensor(f"sum1_{j}", [TABLE_ROWS, ROW], F32) for j in range(TABLES)],
        "sum2": [nc.dram_tensor(f"sum2_{j}", [TABLE_ROWS, COLS2], F32) for j in range(TABLES)],
    }
    with ExitStack() as ctx:
        def sb(name, shape, dt=F32):
            return ctx.enter_context(nc.sbuf_tensor(name, shape, dt))

        keep = {
            "unit": sb("unit", [P, ALL_TILES, XYZ]),
            "recv": sb("recv", [P, ALL_TILES]),
            "sender": sb("sender", [P, ALL_TILES], U32),
            "target": sb("target", [P, ALL_TILES], U32),
            "per_count": sb("per_count", [NODE_PARTS, NODE_COLS]),
            "by_part": sb("by_part", [P, 3]),
            "halves": sb("halves", [2, P], BF16),
            "combine1": sb("combine1", [P, 2, TILES, COLS1]),
        }
        for k in (1, 2):
            keep[f"w1_{k}"] = sb(f"w1_sb_{k}", [P, HK])
            keep[f"b1_{k}"] = sb(f"b1_sb_{k}", [P, 1])
            keep[f"w2_{k}"] = sb(f"w2_sb_{k}", [P, WN])
        constants(nc, keep)
        prepare(nc, a, dram, keep)
        edge_layer(nc, a, dram, keep, 1)
        node_layer(nc, a, dram, keep, 1, dram["node"][:, :])
        edge_layer(nc, a, dram, keep, 2)
        node_layer(nc, a, dram, keep, 2, out)


def _layout(x, src, dst, edge_attr_3, edge_attr_48, w):
    pad = EP - E
    attr = np.concatenate([edge_attr_48, np.zeros((pad, D), edge_attr_48.dtype)])
    vec = np.concatenate([edge_attr_3, np.zeros((pad, XYZ), edge_attr_3.dtype)])
    recv = np.concatenate([src, np.full(pad, PAD_NODE, src.dtype)])
    send = np.concatenate([dst, np.zeros(pad, dst.dtype)])
    cols = lambda v: np.ascontiguousarray(v.reshape(ALL_TILES, P).T)
    part = np.arange(P)
    weight = 3.0 ** (63 - part)
    arrays = {
        "x": x,
        "attr": np.ascontiguousarray(attr.reshape(STEPS, 2, HALF, D).transpose(1, 3, 0, 2)).reshape(2, D, STEPS * HALF),
        "vec": np.ascontiguousarray(vec.reshape(ALL_TILES, P, XYZ).transpose(1, 0, 2)),
        "recv_flat": recv.reshape(P, ALL_TILES),
        "recv_cols": cols(recv),
        "send_cols": cols(send),
        "by_part": np.stack([weight, 2 * weight, FIRST_SPARE + part], 1).astype(np.float32),
    }
    for k in (1, 2):
        f = f"L0_gnn_fc{k - 1}_"
        arrays[f"w1_{k}"] = w[f + "w1"]
        arrays[f"b1_{k}"] = w[f + "b1"].reshape(D, 1)
        for name, v in (("w2", w[f + "w2"]), ("b2", w[f + "b2"].reshape(1, WN))):
            wa = v[:, :NS * NS].reshape(-1, NS, NS)
            wb = v[:, NS * NS:].reshape((-1, NS, NV) if k == 1 else (-1, NV, NS))
            both = np.concatenate([wb, wa], axis=2 if k == 1 else 1)
            arrays[f"{name}_{k}"] = np.ascontiguousarray(both.reshape(-1, WN))
        arrays[f"gs_{k}"], arrays[f"bs_{k}"] = w[f"L0_gnn_bn{k - 1}_gs"], w[f"L0_gnn_bn{k - 1}_bs"]
    arrays["gv_1"] = w["L0_gnn_bn0_gv"]
    return arrays


def kernel(x, src, dst, edge_attr_3, edge_attr_48, **weights):
    import concourse.bacc as _bacc
    from concourse.bass_utils import run_bass_kernel_spmd as _run

    w = {name: np.asarray(v) for name, v in weights.items()}
    arrays = _layout(np.asarray(x), np.asarray(src), np.asarray(dst), np.asarray(edge_attr_3),
                     np.asarray(edge_attr_48), w)
    arrays = {f"in_{name}": np.ascontiguousarray(v) for name, v in arrays.items()}
    nc = _bacc.Bacc("TRN2", target_bir_lowering=False, num_devices=1)
    a = {name[3:]: nc.dram_tensor(name, v.shape, mybir.dt.from_np(v.dtype), kind="ExternalInput").ap()
         for name, v in arrays.items()}
    a["send_cols"] = a["send_cols"].bitcast(U32)
    out = nc.dram_tensor("out_0", [N, NS], F32, kind="ExternalOutput").ap()
    gnn_kernel(nc, a, out)
    r = _run(nc, [arrays], core_ids=[0])
    return r.results[0]["out_0"]
```

```python
from contextlib import ExitStack

import numpy as np

import concourse.bass as bass
from concourse import mybir

F32 = mybir.dt.float32
BF16 = mybir.dt.bfloat16
I32 = mybir.dt.int32
U32 = mybir.dt.uint32
ALU = mybir.AluOpType
ACT = mybir.ActivationFunctionType
AX_X = mybir.AxisListType.X

P = 128
N = 12500
E = 412500
NS, NV, XYZ = 16, 4, 3
D = 3 * NS
HK = D + 1
WN = NS * NS + NS * NV
EPS = 1e-5
TILES = 8
STEP = TILES * P
HALF = STEP // 2
STEPS = -(-E // STEP)
ALL_TILES = STEPS * TILES
EP = STEPS * STEP
PAD_NODE = N
TABLES = TILES
TABLE_ROWS = 12672
WINDOW = P
SENDER_PARTS = 124
FIRST_SPARE = N + 1
NODE_PARTS, NODE_COLS = 125, 100
ROW = 32
PAIRS = TILES // 2
GROUP = 4
HID = 64
assert ROW == 2 * NS and STEPS % 2 == 1 and NODE_PARTS * NODE_COLS == N and TABLE_ROWS >= FIRST_SPARE + P

MSG_T, MSG_S, MSG_V, MSGS = 0, NV, NV + NS, NV + NS + NV * XYZ
ROW_S, ROW_V, ROW_ONE, FIRST = 0, NS, NS + NV * XYZ, ROW
NODE_V, NODE_U, NODE_S = 0, 12, 16
COLS2 = NS


def after(eng, sem, value):
    if not isinstance(value, int) or value > 0:
        eng.wait_ge(sem, value)


def split_in_three(nc, then, x, rest, parts, done):
    then(nc.vector.tensor_copy(parts[0], x))
    then(nc.vector.tensor_tensor(rest, x, parts[0], ALU.subtract))
    then(nc.vector.tensor_copy(parts[1], rest))
    nc.vector.tensor_tensor(parts[2], rest, parts[1], ALU.subtract).then_inc(done, 1)


def prepare(nc, a, dram, keep):
    with ExitStack() as ctx:
        def sb(name, shape, dt):
            return ctx.enter_context(nc.sbuf_tensor(name, shape, dt))

        def sem(name):
            return ctx.enter_context(nc.semaphore(name))

        ZEROS = TABLE_ROWS * COLS2 // P
        zero = sb("zero", [P, ZEROS], F32)
        recv_i = sb("recv_i", [P, ALL_TILES], I32)
        part_i = sb("part_i", [P, ALL_TILES], I32)
        high = sb("high", [P, ALL_TILES], BF16)
        low = sb("low", [P, ALL_TILES], BF16)
        norm2 = sb("norm2", [P, ALL_TILES], F32)
        CHUNKS = 26
        CH = ALL_TILES // CHUNKS
        square = sb("square", [P, CH, XYZ], F32)
        x3 = sb("x3", [NODE_PARTS, NODE_COLS, 3, NS], BF16)
        weight3 = sb("weight3", [P, 3], BF16)
        weight_rest = sb("weight_rest", [P, 1], F32)
        xn = sb("xn", [NODE_PARTS, NODE_COLS, NS], F32)
        xc = sb("xc", [NODE_PARTS, NODE_COLS, NS], F32)
        xq = sb("xq", [NODE_PARTS, NODE_COLS, NS], F32)
        mean = sb("mean", [NODE_PARTS, NODE_COLS], F32)
        var = sb("var", [NODE_PARTS, NODE_COLS], F32)
        std = sb("std", [NODE_PARTS, NODE_COLS], F32)
        rstd = sb("rstd", [NODE_PARTS, NODE_COLS], F32)
        SP_COLS = ALL_TILES // SENDER_PARTS
        BASE_PARTS = 13
        BASE_COLS = STEPS // BASE_PARTS
        send_i = sb("send_i", [SENDER_PARTS, SP_COLS, P], I32)
        send_f = sb("send_f", [SENDER_PARTS, SP_COLS, P], F32)
        send_b = sb("send_b", [SENDER_PARTS, SP_COLS, P], BF16)
        tile_min = sb("tile_min", [SENDER_PARTS, SP_COLS], F32)
        step_min = sb("step_min", [BASE_PARTS, BASE_COLS, TILES], F32)
        base_f = sb("base_f", [BASE_PARTS, BASE_COLS], F32)
        base_i = sb("base_i", [BASE_PARTS, BASE_COLS], I32)
        base_by_tile = sb("base_by_tile", [BASE_PARTS, BASE_COLS, TILES], F32)
        tile_base = sb("tile_base", [SENDER_PARTS, SP_COLS], F32)
        farthest = sb("farthest", [SENDER_PARTS, 1], F32)
        farthest_row = sb("farthest_row", [1, SENDER_PARTS], F32)
        flag = sb("flag", [1, 1], F32)

        x_in, vec_in, recv_in, row_in = sem("x_in"), sem("vec_in"), sem("recv_in"), sem("row_in")
        const_in, zeroed, tables_out = sem("const_in"), sem("zeroed"), sem("tables_out")
        dve_step, split, rows_out = sem("dve_step"), sem("split"), sem("rows_out")
        var_done, std_done, x_done, x_out = sem("var_done"), sem("std_done"), sem("x_done"), sem("x_out")
        norm_done, length_done = sem("norm_done"), sem("length_done")
        send_in, min_done, min_moved = sem("send_in"), sem("min_done"), sem("min_moved")
        base_done, base_moved, place_done = sem("base_done"), sem("base_moved"), sem("place_done")
        weight_done = sem("weight_done")
        place_moved, base_in = sem("place_moved"), sem("base_in")

        with nc.Block() as block:
            @block.sync
            def _(sp):
                sp.dma_start(xn[:], a["x"].rearrange("(p c) k -> p c k", p=NODE_PARTS)).then_inc(x_in, 16)
                sp.dma_start(send_i[:], a["send_flat"]).then_inc(send_in, 16)
                sp.dma_start(recv_i[:], a["recv_flat"]).then_inc(row_in, 16)
                sp.dma_start(keep["unit"][:], a["vec"]).then_inc(vec_in, 16)
                sp.dma_start(keep["sender"][:], a["send_cols"]).then_inc(const_in, 16)
                for k in (1, 2):
                    for h in (0, 64):
                        sp.dma_start(keep[f"w1_{k}"][h:h + D, 0:D], a[f"w1_{k}"]).then_inc(const_in, 16)
                        sp.dma_start(keep[f"b1_{k}"][h:h + D, :], a[f"b1_{k}"]).then_inc(const_in, 16)
                        sp.dma_start(keep[f"w2_{k}"][h:h + D, :], a[f"w2_{k}"]).then_inc(const_in, 16)
                        sp.dma_start(keep[f"w2_{k}"][h + D:h + HK, :], a[f"b2_{k}"]).then_inc(const_in, 16)
                sp.dma_start(keep["by_part"][:], a["by_part"]).then_inc(const_in, 16)
                sp.wait_ge(split, 1)
                sp.dma_start(dram["recv_rows"][0].rearrange("(p t) -> p t", p=P), high[:]).then_inc(rows_out, 16)
                sp.dma_start(dram["recv_rows"][1].rearrange("(p t) -> p t", p=P), low[:]).then_inc(rows_out, 16)
                sp.dma_start(recv_i[:], a["recv_cols"]).then_inc(recv_in, 16)
                sp.wait_ge(zeroed, 1)
                for j in range(TABLES):
                    for h in range(2):
                        sp.dma_start(dram["sum1"][j].rearrange("(p r) k -> p (r k)", p=P)[
                            :, h * ZEROS:(h + 1) * ZEROS], zero[:]).then_inc(tables_out, 16)
                    sp.dma_start(dram["sum2"][j].rearrange("(p r) k -> p (r k)", p=P), zero[:]).then_inc(tables_out, 16)
                sp.wait_ge(x_done, 1)
                sp.dma_start(dram["norm_x"].rearrange("(p c) k -> p c k", p=NODE_PARTS), xc[:]).then_inc(x_out, 16)
                sp.dma_start(dram["norm_x3"].rearrange("(p c) k -> p (c k)", p=NODE_PARTS),
                             x3[:].rearrange("p c h k -> p (c h k)")).then_inc(x_out, 16)
                sp.wait_ge(x_out, 32)
                sp.wait_ge(rows_out, 32)
                sp.wait_ge(place_moved, 32)
                sp.wait_ge(tables_out, 3 * 16 * TABLES)
                sp.wait_ge(const_in, 18 * 16)

            @block.gpsimd
            def _(pool):
                nc.gpsimd.memset(zero[:], 0.0).then_inc(zeroed, 1)

            @block.scalar
            def _(act):
                act.wait_ge(min_done, 1)
                act.dma_start(dram["tile_min"][0:ALL_TILES].rearrange("(p t) -> p t", p=SENDER_PARTS),
                              tile_min[:]).then_inc(min_moved, 16)
                act.wait_ge(min_moved, 16)
                act.dma_start(step_min[:], dram["tile_min"][0:ALL_TILES].rearrange(
                    "(p s t) -> p s t", p=BASE_PARTS, t=TILES)).then_inc(min_moved, 16)
                act.wait_ge(base_done, 1)
                act.dma_start(dram["tile_base"][0:ALL_TILES].rearrange("(p s t) -> p s t", p=BASE_PARTS, t=TILES),
                              base_by_tile[:]).then_inc(base_moved, 16)
                act.dma_start(dram["base"][0:STEPS].rearrange("(p s) -> p s", p=BASE_PARTS),
                              base_i[:]).then_inc(base_moved, 16)
                act.wait_ge(base_moved, 32)
                act.dma_start(tile_base[:], dram["tile_base"][0:ALL_TILES].rearrange(
                    "(p t) -> p t", p=SENDER_PARTS)).then_inc(base_in, 16)
                act.dma_start(keep["base"][:], dram["base"][0:STEPS].rearrange("(o s) -> o s", o=1)).then_inc(base_in, 16)
                act.wait_ge(place_done, 1)
                act.dma_start(dram["place_rows"][0].rearrange("(p t e) -> p t e", p=SENDER_PARTS, e=P),
                              send_b[:]).then_inc(place_moved, 16)
                act.dma_start(dram["farthest"][0:SENDER_PARTS].rearrange("(p o) -> p o", o=1),
                              farthest[:]).then_inc(place_moved, 16)
                act.wait_ge(place_moved, 32)
                act.dma_start(farthest_row[:], dram["farthest"][0:SENDER_PARTS].rearrange(
                    "(o p) -> o p", o=1)).then_inc(base_in, 16)

                act.wait_ge(var_done, 1)
                nc.scalar.activation(std[:], var[:], ACT.Sqrt).then_inc(std_done, 1)
                act.wait_ge(norm_done, CHUNKS)
                nc.scalar.activation(norm2[:], norm2[:], ACT.Sqrt).then_inc(length_done, 1)

            @block.vector
            def _(dve):
                steps = [0]

                def then(ins):
                    steps[0] += 1
                    ins.then_inc(dve_step, 1)
                    dve.wait_ge(dve_step, steps[0])

                per_sender = [SENDER_PARTS, SP_COLS, P]
                dve.wait_ge(send_in, 16)
                then(nc.vector.tensor_copy(send_f[:], send_i[:]))
                nc.vector.tensor_reduce(tile_min[:], send_f[:], AX_X, ALU.min).then_inc(min_done, 1)
                dve.wait_ge(min_moved, 32)
                then(nc.vector.tensor_reduce(base_f[:], step_min[:], AX_X, ALU.min))
                then(nc.vector.tensor_scalar(base_f[:], base_f[:], float(N - WINDOW), None, ALU.min))
                then(nc.vector.tensor_copy(base_i[:], base_f[:]))
                nc.vector.tensor_copy(base_by_tile[:], base_f[:].unsqueeze(2).to_broadcast(
                    [BASE_PARTS, BASE_COLS, TILES])).then_inc(base_done, 1)
                dve.wait_ge(base_in, 32)
                then(nc.vector.tensor_tensor(send_f[:], send_f[:], tile_base[:].unsqueeze(2).to_broadcast(per_sender),
                                             ALU.subtract))
                then(nc.vector.tensor_copy(send_b[:], send_f[:]))
                nc.vector.tensor_reduce(farthest[:], send_f[:].rearrange("p t e -> p (t e)"), AX_X,
                                        ALU.max).then_inc(place_done, 1)

                per_node = [NODE_PARTS, NODE_COLS, NS]
                dve.wait_ge(x_in, 16)
                then(nc.vector.reduce_sum(mean[:], xn[:], AX_X))
                then(nc.vector.tensor_scalar(mean[:], mean[:], 1.0 / NS, None, ALU.mult))
                then(nc.vector.tensor_tensor(xc[:], xn[:], mean[:].unsqueeze(2).to_broadcast(per_node), ALU.subtract))
                then(nc.vector.tensor_tensor(xq[:], xc[:], xc[:], ALU.mult))
                then(nc.vector.reduce_sum(var[:], xq[:], AX_X))
                nc.vector.tensor_scalar(var[:], var[:], 1.0 / NS, EPS, ALU.mult, ALU.add).then_inc(var_done, 1)

                dve.wait_ge(row_in, 16)
                then(nc.vector.tensor_scalar(part_i[:], recv_i[:], 7, None, ALU.logical_shift_right))
                then(nc.vector.tensor_copy(high[:], part_i[:]))
                then(nc.vector.tensor_scalar(part_i[:], recv_i[:], 127, None, ALU.bitwise_and))
                nc.vector.tensor_copy(low[:], part_i[:]).then_inc(split, 1)

                dve.wait_ge(std_done, 1)
                then(nc.vector.reciprocal(rstd[:], std[:]))
                then(nc.vector.tensor_tensor(xc[:], xc[:], rstd[:].unsqueeze(2).to_broadcast(per_node), ALU.mult))
                then(nc.vector.tensor_scalar(xc[:], xc[:], 0.0, None, ALU.max))
                split_in_three(nc, then, xc[:], xq[:], [x3[:, :, h, :] for h in range(3)], x_done)

                dve.wait_ge(const_in, 18 * 16)
                split_in_three(nc, then, keep["by_part"][:, 0:1], weight_rest[:],
                               [weight3[:, h:h + 1] for h in range(3)], weight_done)
                dve.wait_ge(weight_done, 1)
                for h in range(3):
                    then(nc.vector.tensor_copy(keep["parts1"][:, :, h, :, FIRST],
                                               weight3[:, h:h + 1].unsqueeze(2).to_broadcast([P, 2, TILES])))

                unit = keep["unit"]
                dve.wait_ge(vec_in, 16)
                for c in range(CHUNKS):
                    then(nc.vector.tensor_tensor(square[:], unit[:, c * CH:(c + 1) * CH, :],
                                                 unit[:, c * CH:(c + 1) * CH, :], ALU.mult))
                    nc.vector.reduce_sum(norm2[:, c * CH:(c + 1) * CH], square[:], AX_X).then_inc(norm_done, 1)
                    dve.wait_ge(norm_done, c + 1)
                dve.wait_ge(length_done, 1)
                then(nc.vector.tensor_scalar(norm2[:], norm2[:], 1e-12, None, ALU.add))
                then(nc.vector.reciprocal(norm2[:], norm2[:]))
                then(nc.vector.scalar_tensor_tensor(
                    out=unit[:], in0=unit[:], scalar=float(np.sqrt(3.0)),
                    in1=norm2[:].unsqueeze(2).to_broadcast([P, ALL_TILES, XYZ]), op0=ALU.mult, op1=ALU.mult))

                dve.wait_ge(recv_in, 16)
                then(nc.vector.tensor_copy(keep["recv"][:], recv_i[:]))

                dve.wait_ge(base_in, 48)
                then(nc.vector.tensor_reduce(flag[:], farthest_row[:], AX_X, ALU.max))
                then(nc.vector.tensor_scalar(flag[:], flag[:], float(WINDOW - 1), None, ALU.is_le))
                then(nc.vector.tensor_copy(keep["in_windows"][:], flag[:]))


def constants(nc, keep):
    filled = nc.semaphore("filled")
    with filled as filled, nc.Block() as block:
        @block.vector
        def _(dve):
            for k in (1, 2):
                nc.vector.memset(keep[f"w1_{k}"][:], 0.0).then_inc(filled, 1)
                nc.vector.memset(keep[f"b1_{k}"][:], 1.0).then_inc(filled, 1)
                nc.vector.memset(keep[f"w2_{k}"][:], 0.0).then_inc(filled, 1)
            nc.vector.memset(keep["parts1"][:], 0.0).then_inc(filled, 1)
            nc.vector.memset(keep["halves"][:], 1.0).then_inc(filled, 1)
            dve.wait_ge(filled, 8)
            nc.vector.memset(keep["parts1"][:, :, 0, :, ROW_ONE:ROW_ONE + 1], 1.0).then_inc(filled, 1)
            nc.vector.memset(keep["halves"][0:1, :], float(P)).then_inc(filled, 1)
            dve.wait_ge(filled, 10)


def edge_layer(nc, a, dram, keep, layer):
    first = layer == 1
    COLS = FIRST + 1 if first else COLS2
    IN, OUT = (NS, NV + NS) if first else (NV + NS, NS)
    table = dram["norm_x"] if first else dram["node"]
    table3 = dram["norm_x3"] if first else dram["node3"]
    GW = NS if first else ROW
    sums = dram["sum1"] if first else dram["sum2"]
    SW = ROW if first else COLS2
    w1, b1, w2 = (keep[f"{n}_{layer}"] for n in ("w1", "b1", "w2"))
    unit, recv, sender, target = keep["unit"], keep["recv"], keep["sender"], keep["target"]

    with ExitStack() as ctx:
        def sb(name, shape, dt):
            return ctx.enter_context(nc.sbuf_tensor(f"{name}_{layer}", shape, dt))

        def pb(name):
            return ctx.enter_context(nc.psum_tensor(f"{name}_{layer}", [P, 512], F32))

        def sem(name):
            return ctx.enter_context(nc.semaphore(f"{name}_{layer}"))

        def two(name):
            return [sem(f"{name}_even"), sem(f"{name}_odd")]

        attr = sb("attr", [P, 2, HALF], F32)
        recv_row = sb("recv_row", [2, 2, STEP], BF16)
        hidden = sb("hidden", [P, 2, HALF], F32)
        hidden_rest = sb("hidden_rest", [P, HALF], F32)
        hidden_parts = sb("hidden_parts", [P, 2, 3, HALF], BF16)
        stacked = sb("stacked", [P, 2, 2, 2, HALF], BF16)
        w2_parts = sb("w2_parts", [P, 4, WN], BF16)
        w2_rest = sb("w2_rest", [P, WN], F32)
        send_idx = sb("send_idx", [P, 2, TILES], U32)
        target_idx = sb("target_idx", [P, 2, TILES], U32)
        node = sb("node", [P, 2, TILES, GW], F32)
        prod = sb("prod", [P, 2, 2, WN], F32)
        MC = MSGS if first else COLS
        SUMMED = slice(MSG_S, MSGS) if first else slice(0, COLS)
        SN = SUMMED.stop - SUMMED.start
        same = sb("same", [P, 2, STEP], BF16)
        apart = sb("apart", [P, 2, GROUP * P], BF16)
        message = sb("message", [P, 2, TILES, MC], F32)
        rest = sb("rest", [P, TILES, SN], F32)
        parts = keep["parts1"] if first else sb("parts", [P, 2, 3, TILES, COLS], BF16)
        summed = sb("summed", [P, 2, TILES, COLS], F32)
        rows = sb("rows", [P, 2, TILES, SW], F32)
        vdot = sb("vdot", [P, TILES, NV, XYZ], F32)
        shift = sb("shift", [P, TILES], F32)
        window = sb("window", [WINDOW, 2, 3 * GW], BF16)
        place_row = sb("place_row", [P, 2, STEP], BF16)
        at_place = sb("at_place", [WINDOW, 2, STEP], BF16)

        hid_ps = pb("hid_ps")
        weight_ps = ctx.enter_context(nc.psum_tensor(f"weight_ps_{layer}", [P, 2, 2, 512], F32))
        recv_ps = pb("recv_ps")
        comb_ps = pb("comb_ps")
        comb = comb_ps[:, 0:TILES * COLS].rearrange("p (t k) -> p t k", k=COLS)
        node_ps = comb_ps[:, TILES * COLS:TILES * (COLS + GW)].rearrange("p (t k) -> p t k", k=GW)

        gate = sem("gate")
        attr_in = two("attr_in")
        recv_in = two("recv_in")
        stacked_in = two("stacked_in")
        window_in = two("window_in")
        placed = sem("placed")
        picked = sem("picked")
        node_ready = sem("node_ready")
        gathered = two("gathered")
        scattered = [sem(f"scattered{j}") for j in range(TABLES)]
        rows_free = sem("rows_free")
        send_staged = sem("send_staged")
        hid_done = sem("hid_done")
        hidden_ready = sem("hidden_ready")
        hidden_high = sem("hidden_high")
        hidden_less = sem("hidden_less")
        hidden_middle = sem("hidden_middle")
        hidden_low = sem("hidden_low")
        w2_split = sem("w2_split")
        weights_ready = sem("weights_ready")
        weights_used = sem("weights_used")
        reduced = sem("reduced")
        recv_ready = sem("recv_ready")
        apart_done = sem("apart_done")
        same_done = sem("same_done")
        high_done = sem("high_done")
        rest_done = sem("rest_done")
        middle_done = sem("middle_done")
        parts_done = sem("parts_done")
        summed_ready = sem("summed_ready")
        vectors_done = sem("vectors_done")
        comb_done = sem("comb_done")
        rows_ready = sem("rows_ready")
        shift_done = sem("shift_done")
        target_done = sem("target_done")

        class Step:

            def __init__(self, half, odd):
                self.half, self.odd = half, odd
                self.n = half * 2 + odd

            def next(self):
                return Step(self.half, 1) if self.odd == 0 else Step(self.half + 1, 0)

            def prev(self):
                return Step(self.half, 0) if self.odd == 1 else Step(self.half - 1, 1)

            @property
            def has_prev(self):
                return not isinstance(self.n, int) or self.n > 0

            @property
            def has_next(self):
                return not isinstance(self.n, int) or self.n < STEPS - 1

            def cols(self, of, start=0, width=TILES):
                return of[:, bass.ds(self.n * TILES + start, width)]

        def every_step(eng, body):
            for n in range(3):
                body(Step(n // 2, n % 2))
            with eng.Fori(1, STEPS // 2 - 1) as half:
                body(Step(half, 1))
                body(Step(half + 1, 0))
            for n in (STEPS - 2, STEPS - 1):
                body(Step(n // 2, n % 2))

        def both_ways(eng, program):
            flag = eng.value_load(keep["in_windows"][0:1, 0:1], min_val=0, max_val=1)
            with eng.If(flag):
                program(True)
            with eng.Else():
                program(False)

        with nc.Block() as block:
            @block.sync
            def _(sp):
                def program(in_windows):
                    def load_attributes(s):
                        after(sp, hid_done, s.n - 1)
                        sp.sem_inc(gate, 1)
                        for h in range(2):
                            sp.dma_start(attr[HID * h:HID * h + D, s.odd, :],
                                         a["attr"][h][:, bass.ds(s.n * HALF, HALF)]).then_inc(attr_in[s.odd], 16)

                    def load_rows(s):
                        after(sp, recv_ready, (s.n - 1) * (TILES // GROUP))
                        sp.sem_inc(gate, 1)
                        sp.dma_start(recv_row[:, s.odd, :],
                                     dram["recv_rows"][:, bass.ds(s.n * STEP, STEP)]).then_inc(recv_in[s.odd], 16)
                        if in_windows:
                            after(sp, picked, s.n - 1)
                            after(sp, placed, s.n - 1)
                            sp.sem_inc(gate, 1)
                            base = sp.value_load(keep["base"][0:1, bass.ds(s.n, 1)], min_val=0, max_val=N - WINDOW)
                            sp.dma_start(window[:, s.odd, :],
                                         table3[bass.ds(base, WINDOW), :]).then_inc(window_in[s.odd], 16)
                            sp.dma_start(place_row[:, s.odd, :], dram["place_rows"][:, bass.ds(s.n * STEP, STEP)]
                                         .to_broadcast([P, STEP])).then_inc(window_in[s.odd], 16)

                    def stack(s):
                        after(sp, hidden_low, s.n + 1)
                        sp.sem_inc(gate, 1)
                        after(sp, weights_ready, PAIRS * (s.n - 1))
                        sp.sem_inc(gate, 1)
                        for h in range(2):
                            here, there = slice(HID * h, HID * h + HID), slice(HID - HID * h, P - HID * h)
                            sp.dma_start(stacked[here, s.odd, h, :, :], hidden_parts[here, s.odd, 0:1, :]
                                         .to_broadcast([HID, 2, HALF])).then_inc(stacked_in[s.odd], 16)
                            sp.dma_start(stacked[there, s.odd, h, :, :],
                                         hidden_parts[here, s.odd, 1:3, :]).then_inc(stacked_in[s.odd], 16)

                    def body(s):
                        if s.has_next and s.next().has_next:
                            load_attributes(s.next().next())
                        if s.has_next:
                            stack(s.next())
                        if s.has_next and s.next().has_next:
                            load_rows(s.next().next())

                    for s in (Step(0, 0), Step(0, 1)):
                        load_attributes(s)
                        load_rows(s)
                    stack(Step(0, 0))
                    every_step(sp, body)

                both_ways(sp, program)

            @block.gpsimd
            def _(pool):
                def program(in_windows):
                    def gather(s):
                        after(pool, send_staged, s.n + 1)
                        after(pool, weights_used, PAIRS * (s.n - 1))
                        pool.sem_inc(gate, 1)
                        for j in range(TILES):
                            nc.gpsimd.indirect_dma_start(
                                node[:, s.odd, j, :], None, table[:, :],
                                bass.IndirectOffsetOnAxis(send_idx[:, s.odd, j:j + 1], 0),
                            ).then_inc(gathered[s.odd], 16)

                    def scatter(s):
                        after(pool, rows_ready, 2 * (s.n + 1))
                        for j in range(TABLES):
                            after(pool, scattered[j], s.n * 16)
                        pool.sem_inc(rows_free, 1)
                        for j in range(TABLES):
                            nc.gpsimd.indirect_dma_start(
                                sums[j][:, :], bass.IndirectOffsetOnAxis(target_idx[:, s.odd, j:j + 1], 0),
                                rows[:, s.odd, j, :], None, compute_op=ALU.add,
                            ).then_inc(scattered[j], 16)

                    def body(s):
                        if s.has_next and not in_windows:
                            gather(s.next())
                        if s.has_prev and s.prev().has_prev:
                            scatter(s.prev().prev())

                    if not in_windows:
                        gather(Step(0, 0))
                    every_step(pool, body)
                    scatter(Step(STEPS // 2 - 1, 1))
                    scatter(Step(STEPS // 2, 0))
                    for j in range(TABLES):
                        pool.wait_ge(scattered[j], STEPS * 16)

                both_ways(pool, program)

            @block.scalar
            def _(act):
                def program(in_windows):
                    def stage_sender(s):
                        after(act, gathered[s.odd], s.half * TILES * 16)
                        nc.scalar.copy(send_idx[:, s.odd, :], s.cols(sender)).then_inc(send_staged, 1)

                    def move_nodes(s):
                        after(act, picked, s.n + 1)
                        after(act, comb_done, s.n - 1)
                        after(act, weights_used, PAIRS * (s.n - 1))
                        nc.scalar.copy(node[:, s.odd, :, :], node_ps).then_inc(node_ready, 1)

                    def relu(s):
                        after(act, hid_done, s.n + 1)
                        after(act, hidden_less, s.n - 1)
                        nc.scalar.activation(hidden[:, s.odd, :], hid_ps[:, :], ACT.Relu,
                                             bias=b1[:, :]).then_inc(hidden_ready, 1)

                    def hidden_high_part(s):
                        after(act, hidden_ready, s.n + 1)
                        after(act, stacked_in[s.odd], s.half * 4 * 16)
                        nc.scalar.copy(hidden_parts[:, s.odd, 0, :], hidden[:, s.odd, :]).then_inc(hidden_high, 1)

                    def hidden_middle_part(s):
                        after(act, hidden_less, s.n + 1)
                        nc.scalar.copy(hidden_parts[:, s.odd, 1, :], hidden_rest[:]).then_inc(hidden_middle, 1)

                    def equal_receivers(s, c):
                        after(act, recv_ready, 2 * s.n + c + 1)
                        after(act, same_done, 2 * s.n + c - 1)
                        for t in range(GROUP):
                            nc.scalar.activation(
                                apart[:, c, t * P:(t + 1) * P], recv_ps[:, t * P:(t + 1) * P], ACT.Square,
                                bias=s.cols(recv, c * GROUP + t, 1), scale=-1.0).then_inc(apart_done, 1)
                        after(act, apart_done, GROUP * (2 * s.n + c + 1))
                        after(act, comb_done, s.n - 1)
                        nc.scalar.activation(same[:, s.odd, c * GROUP * P:(c + 1) * GROUP * P], apart[:, c, :],
                                             ACT.Relu, bias=1.0, scale=-1.0).then_inc(same_done, 1)

                    def high_part(s):
                        after(act, *((vectors_done, s.n + 1) if first else (reduced, PAIRS * (s.n + 1))))
                        after(act, comb_done, s.n - 1)
                        nc.scalar.copy(parts[:, s.odd, 0, :, 0:SN], message[:, s.odd, :, SUMMED]).then_inc(high_done, 1)

                    def middle_part(s):
                        after(act, rest_done, s.n + 1)
                        nc.scalar.copy(parts[:, s.odd, 1, :, 0:SN], rest[:]).then_inc(middle_done, 1)

                    def move_sums(s):
                        after(act, rows_ready, 2 * (s.n - 1))
                        after(act, comb_done, s.n + 1)
                        nc.scalar.copy(summed[:, s.odd, :, :], comb).then_inc(summed_ready, 1)

                    def stage_rows(s):
                        after(act, rows_free, s.n)
                        after(act, summed_ready, s.n + 1)
                        nc.scalar.copy(rows[:, s.odd, :, :], summed[:, s.odd, :, 0:SW]).then_inc(rows_ready, 1)
                        if first:
                            after(act, target_done, s.n + 1)
                        nc.scalar.copy(target_idx[:, s.odd, :], s.cols(target)).then_inc(rows_ready, 1)

                    def body(s):
                        if s.has_prev:
                            high_part(s.prev())
                        if s.has_next and not in_windows:
                            stage_sender(s.next())
                        equal_receivers(s, 0)
                        if s.has_prev:
                            middle_part(s.prev())
                        if s.has_next and s.next().has_next:
                            relu(s.next().next())
                            hidden_high_part(s.next().next())
                        equal_receivers(s, 1)
                        if s.has_next and s.next().has_next:
                            hidden_middle_part(s.next().next())
                        if s.has_prev and s.prev().has_prev:
                            stage_rows(s.prev().prev())
                        if s.has_next and in_windows:
                            move_nodes(s.next())
                        if s.has_prev:
                            move_sums(s.prev())

                    for s in (Step(0, 0), Step(0, 1)):
                        relu(s)
                        hidden_high_part(s)
                        hidden_middle_part(s)
                    if in_windows:
                        move_nodes(Step(0, 0))
                    else:
                        stage_sender(Step(0, 0))
                    every_step(act, body)
                    last = Step(STEPS // 2, 0)
                    high_part(last)
                    middle_part(last)
                    stage_rows(last.prev())
                    move_sums(last)
                    stage_rows(last)

                both_ways(act, program)

            @block.tensor
            def _(pe):
                def program(in_windows):
                    def hidden_product(s):
                        after(pe, attr_in[s.odd], (s.half + 1) * 2 * 16)
                        after(pe, hidden_ready, s.n)
                        pe.sem_inc(gate, 1)
                        for h in range(2):
                            lo = HID * h
                            mm = nc.tensor.matmul(hid_ps[lo:lo + HID, :], w1[lo:lo + D, :],
                                                  attr[lo:lo + D, s.odd, :], start=True, stop=True)
                        mm.then_inc(hid_done, 1)

                    def weight_product(s, j):
                        if j == 0:
                            after(pe, stacked_in[s.odd], (s.half + 1) * 4 * 16)
                        after(pe, weights_used, PAIRS * s.n + j - 1)
                        pe.sem_inc(gate, 1)
                        for h in range(2):
                            for n, (x, w) in enumerate(((0, 0), (0, 1), (1, 2 + h))):
                                mm = nc.tensor.matmul(weight_ps[:, j % 2, h, 0:WN],
                                                      stacked[:, s.odd, h, x, j * P:(j + 1) * P],
                                                      w2_parts[:, w, :], start=(n == 0), stop=(n == 2))
                        mm.then_inc(weights_ready, 1)

                    def pick_nodes(s):
                        after(pe, placed, s.n + 1)
                        after(pe, window_in[s.odd], (s.half + 1) * 2 * 16)
                        after(pe, node_ready, s.n)
                        after(pe, summed_ready, s.n - 2)
                        for t in range(TILES):
                            for h in range(3):
                                mm = nc.tensor.matmul(node_ps[:, t, :], at_place[:, s.odd, t * P:(t + 1) * P],
                                                      window[:, s.odd, h * GW:(h + 1) * GW],
                                                      start=(h == 0), stop=(h == 2))
                        mm.then_inc(picked, 1)

                    def receivers(s, c):
                        after(pe, recv_in[s.odd], (s.half + 1) * 16)
                        after(pe, apart_done, GROUP * (2 * s.n + c))
                        nc.tensor.matmul(recv_ps[:, :], keep["halves"][:, :],
                                         recv_row[:, s.odd, c * GROUP * P:(c + 1) * GROUP * P],
                                         start=True, stop=True).then_inc(recv_ready, 1)

                    def combine_messages(s):
                        after(pe, same_done, 2 * s.n + 2)
                        after(pe, parts_done, s.n + 1)
                        after(pe, summed_ready, s.n)
                        for t in range(TILES):
                            for h in range(3):
                                mm = nc.tensor.matmul(comb[:, t, :], same[:, s.odd, t * P:(t + 1) * P],
                                                      parts[:, s.odd, h, t, :], start=(h == 0), stop=(h == 2))
                        mm.then_inc(comb_done, 1)

                    def body(s):
                        weight_product(s, 0)
                        receivers(s, 0)
                        weight_product(s, 1)
                        if s.has_next and s.next().has_next:
                            hidden_product(s.next().next())
                        receivers(s, 1)
                        weight_product(s, 2)
                        weight_product(s, 3)
                        if s.has_next and in_windows:
                            pick_nodes(s.next())
                        if s.has_prev:
                            combine_messages(s.prev())

                    for s in (Step(0, 0), Step(0, 1)):
                        hidden_product(s)
                    if in_windows:
                        pick_nodes(Step(0, 0))
                    pe.wait_ge(w2_split, 7)
                    every_step(pe, body)
                    combine_messages(Step(STEPS // 2, 0))

                both_ways(pe, program)

            @block.vector
            def _(dve):
                def split_w2():
                    lower, upper = slice(0, HID), slice(HID, P)
                    nc.vector.tensor_copy(w2_parts[:, 0, :], w2[:]).then_inc(w2_split, 1)
                    dve.wait_ge(w2_split, 1)
                    nc.vector.tensor_tensor(w2_rest[:], w2[:], w2_parts[:, 0, :], ALU.subtract).then_inc(w2_split, 1)
                    dve.wait_ge(w2_split, 2)
                    nc.vector.tensor_copy(w2_parts[:, 1, :], w2_rest[:]).then_inc(w2_split, 1)
                    dve.wait_ge(w2_split, 3)
                    for low, high, n in ((lower, upper, 2), (upper, lower, 3)):
                        nc.vector.tensor_tensor(w2_parts[low, n, :], w2_rest[low, :], w2_parts[low, 1, :],
                                                ALU.subtract).then_inc(w2_split, 1)
                        nc.vector.tensor_copy(w2_parts[high, n, :], w2_parts[high, 0, :]).then_inc(w2_split, 1)

                def program(in_windows):
                    def hidden_rest_part(s):
                        dve.wait_ge(hidden_high, s.n + 1)
                        after(dve, hidden_low, s.n)
                        nc.vector.tensor_tensor(hidden_rest[:], hidden[:, s.odd, :], hidden_parts[:, s.odd, 0, :],
                                                ALU.subtract).then_inc(hidden_less, 1)

                    def hidden_low_part(s):
                        dve.wait_ge(hidden_middle, s.n + 1)
                        nc.vector.tensor_tensor(hidden_parts[:, s.odd, 2, :], hidden_rest[:],
                                                hidden_parts[:, s.odd, 1, :], ALU.subtract).then_inc(hidden_low, 1)

                    def vector_inputs(s):
                        if s.has_prev:
                            dve.wait_ge(vectors_done, s.n * 2)
                        nc.vector.tensor_tensor(
                            vdot[:], node[:, s.odd, :, NODE_V:NODE_V + NV * XYZ].rearrange("p t (j c) -> p t j c", c=XYZ),
                            s.cols(unit).unsqueeze(2).to_broadcast([P, TILES, NV, XYZ]),
                            ALU.mult).then_inc(vectors_done, 1)
                        dve.wait_ge(vectors_done, s.n * 2 + 1)
                        nc.vector.reduce_sum(node[:, s.odd, :, NODE_U:NODE_U + NV], vdot[:], AX_X).then_inc(vectors_done, 1)
                        dve.wait_ge(vectors_done, s.n * 2 + 2)

                    def product(s, j):
                        dve.wait_ge(weights_ready, PAIRS * s.n + j + 1)
                        after(dve, reduced, PAIRS * s.n + j - 1)
                        w = weight_ps[:, j % 2, :, 0:WN].rearrange("p h (i o) -> p h i o", o=OUT)
                        x = node[:, s.odd, :, GW - IN:GW].rearrange("p (h j) i -> p h j i", h=2)[:, :, j, :]
                        nc.vector.tensor_tensor(
                            prod[:, j % 2, :, :].rearrange("p h (i o) -> p h i o", o=OUT), w,
                            x.unsqueeze(3).to_broadcast([P, 2, IN, OUT]), ALU.mult).then_inc(weights_used, 1)

                    def reduce(s, j):
                        dve.wait_ge(weights_used, PAIRS * s.n + j + 1)
                        out = message[:, s.odd, :, 0:OUT].rearrange("p (h j) o -> p h j o", h=2)[:, :, j, :]
                        nc.vector.reduce_sum(out, prod[:, j % 2, :, :].rearrange("p h (i o) -> p h o i", o=OUT),
                                             AX_X).then_inc(reduced, 1)

                    def place(s):
                        dve.wait_ge(window_in[s.odd], (s.half + 1) * 2 * 16)
                        after(dve, picked, s.n - 1)
                        nc.vector.tensor_scalar(at_place[:, s.odd, :], place_row[:, s.odd, :],
                                                keep["by_part"][:, 3:4], None, ALU.is_equal).then_inc(placed, 1)

                    def rest_part(s):
                        dve.wait_ge(high_done, s.n + 1)
                        after(dve, parts_done, s.n)
                        nc.vector.tensor_tensor(rest[:], message[:, s.odd, :, SUMMED], parts[:, s.odd, 0, :, 0:SN],
                                                ALU.subtract).then_inc(rest_done, 1)

                    def low_part(s):
                        dve.wait_ge(middle_done, s.n + 1)
                        nc.vector.tensor_tensor(parts[:, s.odd, 2, :, 0:SN], rest[:], parts[:, s.odd, 1, :, 0:SN],
                                                ALU.subtract).then_inc(parts_done, 1)

                    def vector_messages(s):
                        dve.wait_ge(reduced, PAIRS * (s.n + 1))
                        nc.vector.tensor_tensor(
                            message[:, s.odd, :, MSG_V:MSGS].rearrange("p t (j c) -> p t j c", c=XYZ),
                            message[:, s.odd, :, MSG_T:MSG_T + NV].unsqueeze(3).to_broadcast([P, TILES, NV, XYZ]),
                            s.cols(unit).unsqueeze(2).to_broadcast([P, TILES, NV, XYZ]),
                            ALU.mult).then_inc(vectors_done, 1)

                    def targets(s):
                        by_part = keep["by_part"]
                        dve.wait_ge(summed_ready, s.n + 1)
                        nc.vector.tensor_scalar(shift[:], s.cols(recv), -1.0, by_part[:, 2:3],
                                                ALU.mult, ALU.add).then_inc(shift_done, 1)
                        dve.wait_ge(shift_done, 2 * s.n + 1)
                        nc.vector.scalar_tensor_tensor(out=shift[:], in0=summed[:, s.odd, :, FIRST], scalar=by_part[:, 1:2],
                                                       in1=shift[:], op0=ALU.is_gt, op1=ALU.mult).then_inc(shift_done, 1)
                        dve.wait_ge(shift_done, 2 * s.n + 2)
                        nc.vector.tensor_tensor(s.cols(target), s.cols(recv), shift[:], ALU.add).then_inc(target_done, 1)

                    def body(s):
                        if in_windows:
                            dve.wait_ge(node_ready, s.n + 1)
                        else:
                            dve.wait_ge(gathered[s.odd], (s.half + 1) * TILES * 16)
                        if not first:
                            vector_inputs(s)
                        product(s, 0)
                        if s.has_prev:
                            rest_part(s.prev())
                        product(s, 1)
                        reduce(s, 0)
                        if s.has_next and in_windows:
                            place(s.next())
                        if s.has_prev:
                            low_part(s.prev())
                        product(s, 2)
                        reduce(s, 1)
                        if s.has_next and s.next().has_next:
                            hidden_rest_part(s.next().next())
                        product(s, 3)
                        reduce(s, 2)
                        if first and s.has_prev and s.prev().has_prev:
                            targets(s.prev().prev())
                        if s.has_next and s.next().has_next:
                            hidden_low_part(s.next().next())
                        reduce(s, 3)
                        if first:
                            vector_messages(s)

                    for s in (Step(0, 0), Step(0, 1)):
                        hidden_rest_part(s)
                        hidden_low_part(s)
                    if in_windows:
                        place(Step(0, 0))
                    every_step(dve, body)
                    last = Step(STEPS // 2, 0)
                    rest_part(last)
                    low_part(last)
                    if first:
                        targets(last.prev())
                        targets(last)

                split_w2()
                both_ways(dve, program)

def node_layer(nc, a, dram, keep, layer, out):
    first = layer == 1
    sums, W = (dram["sum1"], ROW) if first else (dram["sum2"], COLS2)
    SCALE = 1.0 / np.sqrt(NS) if first else 1.0 / np.sqrt(NS + NV)
    S_AT = ROW_S if first else 0
    BUFS = 3
    PN, CN = NODE_PARTS, NODE_COLS
    with ExitStack() as ctx:
        def sb(name, shape, dt=F32):
            return ctx.enter_context(nc.sbuf_tensor(f"{name}_n{layer}", shape, dt))

        def sem(name):
            return ctx.enter_context(nc.semaphore(f"{name}_n{layer}"))

        total = sb("total", [PN, CN, W])
        part = sb("part", [PN, BUFS, CN * W])
        square = sb("square", [PN, CN, NS])
        ones = sb("ones", [PN, P])
        gain, bias = sb("gain", [PN, NS]), sb("bias", [PN, NS])
        vgain = sb("vgain", [PN, NV])
        colsum = sb("colsum", [PN, NS])
        mean = sb("mean", [PN, NS])
        var = sb("var", [PN, NS])
        std = sb("std", [PN, NS])
        result = sb("result", [PN, CN, ROW if first else NS])
        result3 = sb("result3", [PN, CN, 3, ROW if first else 1], BF16)
        rest = sb("rest", [PN, CN, ROW if first else 1])
        x_old = sb("x_old", [PN, CN, NS])
        stat_ps = ctx.enter_context(nc.psum_tensor(f"stat_ps_n{layer}", [P, 512], F32))
        table_in = [sem(f"table_in{b}") for b in range(BUFS)]
        total_in, par_in, ones_done, x_in = sem("total_in"), sem("par_in"), sem("ones_done"), sem("x_in")
        added, step, colsum_done, stat_done = sem("added"), sem("step"), sem("colsum_done"), sem("stat_done")
        var_done, std_done, result_done, result_out = (
            sem("var_done"), sem("std_done"), sem("result_done"), sem("result_out"))
        STATS = 3 if first else 2

        with nc.Block() as block:
            @block.sync
            def _(sp):
                def table_of(j):
                    return sums[j][0:N, :].rearrange("(p c) k -> p (c k)", p=PN)

                def row_of(v, n):
                    return v.rearrange("(o k) -> o k", o=1).to_broadcast([PN, n])

                sp.dma_start(total[:].rearrange("p c k -> p (c k)"), table_of(0)).then_inc(total_in, 16)
                for j in range(1, TABLES):
                    after(sp, added, j - BUFS)
                    sp.dma_start(part[:, j % BUFS, :], table_of(j)).then_inc(table_in[j % BUFS], 16)
                sp.dma_start(gain[:], row_of(a[f"gs_{layer}"], NS)).then_inc(par_in, 16)
                sp.dma_start(bias[:], row_of(a[f"bs_{layer}"], NS)).then_inc(par_in, 16)
                if first:
                    sp.dma_start(vgain[:], row_of(a["gv_1"], NV)).then_inc(par_in, 16)
                else:
                    sp.dma_start(x_old[:], a["x"].rearrange("(p c) k -> p c k", p=PN)).then_inc(x_in, 16)
                sp.wait_ge(result_done, 1)
                sp.dma_start(out.rearrange("(p c) k -> p c k", p=PN), result[:]).then_inc(result_out, 16)
                if first:
                    sp.dma_start(dram["node3"].rearrange("(p c) k -> p (c k)", p=PN),
                                 result3[:].rearrange("p c h k -> p (c h k)")).then_inc(result_out, 16)
                sp.wait_ge(result_out, 32 if first else 16)

            @block.gpsimd
            def _(pool):
                nc.gpsimd.memset(ones[:], 1.0).then_inc(ones_done, 1)

            @block.tensor
            def _(pe):
                pe.wait_ge(ones_done, 1)
                for n in range(STATS):
                    k = NS if n < 2 else NV
                    pe.wait_ge(colsum_done, n + 1)
                    nc.tensor.matmul(stat_ps[0:PN, n * NS:n * NS + k], ones[:, 0:PN], colsum[:, 0:k],
                                     start=True, stop=True).then_inc(stat_done, 1)

            @block.scalar
            def _(act):
                for n in range(STATS - 1):
                    k = NS if n < 1 else NV
                    act.wait_ge(var_done, n + 1)
                    nc.scalar.activation(std[:, 0:k], var[:, 0:k], ACT.Sqrt).then_inc(std_done, 1)

            @block.vector
            def _(dve):
                steps = [0]

                def then(ins):
                    steps[0] += 1
                    ins.then_inc(step, 1)
                    dve.wait_ge(step, steps[0])

                def over_nodes(v, k):
                    return v[:, 0:k].unsqueeze(1).to_broadcast([PN, CN, k])

                flat = total[:].rearrange("p c k -> p (c k)")
                dve.wait_ge(total_in, 16)
                for j in range(1, TABLES):
                    dve.wait_ge(table_in[j % BUFS], 16 * ((j - (j % BUFS or BUFS)) // BUFS + 1))
                    nc.vector.tensor_tensor(flat, flat, part[:, j % BUFS, :], ALU.add).then_inc(added, 1)
                    dve.wait_ge(added, j)
                per_count = keep["per_count"]
                if first:
                    then(nc.vector.tensor_scalar(per_count[:], total[:, :, ROW_ONE], 1.0, None, ALU.max))
                    then(nc.vector.reciprocal(per_count[:], per_count[:]))
                then(nc.vector.scalar_tensor_tensor(
                    out=total[:], in0=total[:], scalar=float(SCALE),
                    in1=per_count[:].unsqueeze(2).to_broadcast([PN, CN, W]), op0=ALU.mult, op1=ALU.mult))
                s = total[:, :, S_AT:S_AT + NS]
                nc.vector.reduce_sum(colsum[:], s.rearrange("p c k -> p k c"), AX_X).then_inc(colsum_done, 1)
                dve.wait_ge(stat_done, 1)
                then(nc.vector.tensor_scalar(mean[:], stat_ps[0:PN, 0:NS], 1.0 / N, None, ALU.mult))
                then(nc.vector.tensor_tensor(s, s, over_nodes(mean, NS), ALU.subtract))
                then(nc.vector.tensor_tensor(square[:], s, s, ALU.mult))
                nc.vector.reduce_sum(colsum[:], square[:].rearrange("p c k -> p k c"), AX_X).then_inc(colsum_done, 1)
                dve.wait_ge(stat_done, 2)
                nc.vector.tensor_scalar(var[:], stat_ps[0:PN, NS:2 * NS], 1.0 / N, EPS,
                                        ALU.mult, ALU.add).then_inc(var_done, 1)
                dve.wait_ge(std_done, 1)
                dve.wait_ge(par_in, 48 if first else 32)
                then(nc.vector.reciprocal(mean[:], std[:]))
                then(nc.vector.tensor_tensor(gain[:], gain[:], mean[:], ALU.mult))
                then(nc.vector.tensor_tensor(s, s, over_nodes(gain, NS), ALU.mult))
                if not first:
                    dve.wait_ge(x_in, 16)
                    then(nc.vector.tensor_tensor(s, s, over_nodes(bias, NS), ALU.add))
                    nc.vector.tensor_tensor(result[:], x_old[:], s, ALU.add).then_inc(result_done, 1)
                    return
                then(nc.vector.memset(result[:, :, NODE_U:NODE_S], 0.0))
                then(nc.vector.tensor_tensor(result[:, :, NODE_S:ROW], s, over_nodes(bias, NS), ALU.add))
                v = total[:, :, ROW_V:ROW_V + NV * XYZ]
                then(nc.vector.tensor_tensor(square[:, :, 0:NV * XYZ], v, v, ALU.mult))
                vsum = colsum[:, NV:NV + NV * XYZ]
                then(nc.vector.reduce_sum(vsum, square[:, :, 0:NV * XYZ].rearrange("p c k -> p k c"), AX_X))
                nc.vector.reduce_sum(colsum[:, 0:NV], vsum.rearrange("p (j c) -> p j c", c=XYZ),
                                     AX_X).then_inc(colsum_done, 1)
                dve.wait_ge(stat_done, 3)
                nc.vector.tensor_scalar(var[:, 0:NV], stat_ps[0:PN, 2 * NS:2 * NS + NV], 1.0 / (XYZ * N), EPS,
                                        ALU.mult, ALU.add).then_inc(var_done, 1)
                dve.wait_ge(std_done, 2)
                then(nc.vector.reciprocal(mean[:, 0:NV], std[:, 0:NV]))
                then(nc.vector.scalar_tensor_tensor(out=vgain[:], in0=vgain[:], scalar=float(1.0 / np.sqrt(3.0)),
                                                    in1=mean[:, 0:NV], op0=ALU.mult, op1=ALU.mult))
                then(nc.vector.tensor_copy(mean[:, 0:NV * XYZ].rearrange("p (j c) -> p j c", c=XYZ),
                                           vgain[:].unsqueeze(2).to_broadcast([PN, NV, XYZ])))
                then(nc.vector.tensor_tensor(result[:, :, NODE_V:NODE_V + NV * XYZ], v, over_nodes(mean, NV * XYZ),
                                             ALU.mult))
                split_in_three(nc, then, result[:], rest[:], [result3[:, :, h, :] for h in range(3)], result_done)


def gnn_kernel(nc, a, out):
    dram = {
        "norm_x": nc.dram_tensor("norm_x", [N, NS], F32),
        "norm_x3": nc.dram_tensor("norm_x3", [N, 3 * NS], BF16),
        "node3": nc.dram_tensor("node3", [N, 3 * ROW], BF16),
        "node": nc.dram_tensor("node", [N, ROW], F32),
        "place_rows": nc.dram_tensor("place_rows", [1, EP], BF16),
        "tile_min": nc.dram_tensor("tile_min_d", [ALL_TILES], F32),
        "tile_base": nc.dram_tensor("tile_base_d", [ALL_TILES], F32),
        "base": nc.dram_tensor("base_d", [STEPS], I32),
        "farthest": nc.dram_tensor("farthest_d", [SENDER_PARTS], F32),
        "recv_rows": nc.dram_tensor("recv_rows", [2, EP], BF16),
        "sum1": [nc.dram_tensor(f"sum1_{j}", [TABLE_ROWS, ROW], F32) for j in range(TABLES)],
        "sum2": [nc.dram_tensor(f"sum2_{j}", [TABLE_ROWS, COLS2], F32) for j in range(TABLES)],
    }
    with ExitStack() as ctx:
        def sb(name, shape, dt=F32):
            return ctx.enter_context(nc.sbuf_tensor(name, shape, dt))

        keep = {
            "unit": sb("unit", [P, ALL_TILES, XYZ]),
            "recv": sb("recv", [P, ALL_TILES]),
            "sender": sb("sender", [P, ALL_TILES], U32),
            "target": sb("target", [P, ALL_TILES], U32),
            "per_count": sb("per_count", [NODE_PARTS, NODE_COLS]),
            "by_part": sb("by_part", [P, 4]),
            "base": sb("base", [1, STEPS], I32),
            "in_windows": sb("in_windows", [1, 1], I32),
            "halves": sb("halves", [2, P], BF16),
            "parts1": sb("parts1", [P, 2, 3, TILES, FIRST + 1], BF16),
        }
        for k in (1, 2):
            keep[f"w1_{k}"] = sb(f"w1_sb_{k}", [P, HID])
            keep[f"b1_{k}"] = sb(f"b1_sb_{k}", [P, 1])
            keep[f"w2_{k}"] = sb(f"w2_sb_{k}", [P, WN])
        constants(nc, keep)
        prepare(nc, a, dram, keep)
        edge_layer(nc, a, dram, keep, 1)
        node_layer(nc, a, dram, keep, 1, dram["node"][:, :])
        edge_layer(nc, a, dram, keep, 2)
        node_layer(nc, a, dram, keep, 2, out)


def _layout(x, src, dst, edge_attr_3, edge_attr_48, w):
    pad = EP - E
    attr = np.concatenate([edge_attr_48, np.zeros((pad, D), edge_attr_48.dtype)])
    vec = np.concatenate([edge_attr_3, np.zeros((pad, XYZ), edge_attr_3.dtype)])
    recv = np.concatenate([src, np.full(pad, PAD_NODE, src.dtype)])
    send = np.concatenate([dst, np.repeat(dst[-1:], pad)])
    cols = lambda v: np.ascontiguousarray(v.reshape(ALL_TILES, P).T)
    part = np.arange(P)
    weight = 3.0 ** (63 - part)
    arrays = {
        "x": x,
        "attr": np.ascontiguousarray(attr.reshape(STEPS, 2, HALF, D).transpose(1, 3, 0, 2)).reshape(2, D, STEPS * HALF),
        "vec": np.ascontiguousarray(vec.reshape(ALL_TILES, P, XYZ).transpose(1, 0, 2)),
        "recv_flat": recv.reshape(P, ALL_TILES),
        "recv_cols": cols(recv),
        "send_flat": send.reshape(SENDER_PARTS, ALL_TILES // SENDER_PARTS, P),
        "send_cols": cols(send),
        "by_part": np.stack([weight, 2 * weight, FIRST_SPARE + part, part], 1).astype(np.float32),
    }
    for k in (1, 2):
        f = f"L0_gnn_fc{k - 1}_"
        arrays[f"w1_{k}"] = w[f + "w1"]
        arrays[f"b1_{k}"] = w[f + "b1"].reshape(D, 1)
        for name, v in (("w2", w[f + "w2"]), ("b2", w[f + "b2"].reshape(1, WN))):
            wa = v[:, :NS * NS].reshape(-1, NS, NS)
            wb = v[:, NS * NS:].reshape((-1, NS, NV) if k == 1 else (-1, NV, NS))
            both = np.concatenate([wb, wa], axis=2 if k == 1 else 1)
            arrays[f"{name}_{k}"] = np.ascontiguousarray(both.reshape(-1, WN))
        arrays[f"gs_{k}"], arrays[f"bs_{k}"] = w[f"L0_gnn_bn{k - 1}_gs"], w[f"L0_gnn_bn{k - 1}_bs"]
    arrays["gv_1"] = w["L0_gnn_bn0_gv"]
    return arrays


def kernel(x, src, dst, edge_attr_3, edge_attr_48, **weights):
    import concourse.bacc as _bacc
    from concourse.bass_utils import run_bass_kernel_spmd as _run

    w = {name: np.asarray(v) for name, v in weights.items()}
    arrays = _layout(np.asarray(x), np.asarray(src), np.asarray(dst), np.asarray(edge_attr_3),
                     np.asarray(edge_attr_48), w)
    arrays = {f"in_{name}": np.ascontiguousarray(v) for name, v in arrays.items()}
    nc = _bacc.Bacc("TRN2", target_bir_lowering=False, num_devices=1)
    a = {name[3:]: nc.dram_tensor(name, v.shape, mybir.dt.from_np(v.dtype), kind="ExternalInput").ap()
         for name, v in arrays.items()}
    a["send_cols"] = a["send_cols"].bitcast(U32)
    out = nc.dram_tensor("out_0", [N, NS], F32, kind="ExternalOutput").ap()
    gnn_kernel(nc, a, out)
    r = _run(nc, [arrays], core_ids=[0])
    return r.results[0]["out_0"]
```

```python
from contextlib import ExitStack

import numpy as np

import concourse.bass as bass
from concourse import mybir

F32 = mybir.dt.float32
BF16 = mybir.dt.bfloat16
I32 = mybir.dt.int32
U32 = mybir.dt.uint32
ALU = mybir.AluOpType
ACT = mybir.ActivationFunctionType
AX_X = mybir.AxisListType.X

P = 128
N = 12500
E = 412500
NS, NV, XYZ = 16, 4, 3
D = 3 * NS
HK = D + 1
WN = NS * NS + NS * NV
EPS = 1e-5
TILES = 8
STEP = TILES * P
HALF = STEP // 2
STEPS = -(-E // STEP)
ALL_TILES = STEPS * TILES
EP = STEPS * STEP
PAD_NODE = N
TABLES = TILES
TABLE_ROWS = 12672
WINDOW = P
SENDER_PARTS = 124
FIRST_SPARE = N + 1
NODE_PARTS, NODE_COLS = 125, 100
ROW = 32
PAIRS = TILES // 2
ASK_ALL = 3
GROUP = 4
HID = 64
assert ROW == 2 * NS and STEPS % 2 == 1 and NODE_PARTS * NODE_COLS == N and TABLE_ROWS >= FIRST_SPARE + P

ROW_S, ROW_V, ROW_ONE, FIRST = 0, NS, NS + NV * XYZ, ROW
MSG_T, MSG_S = 0, NV
MSG_V, MSG_V_END = MSG_S + ROW_V, MSG_S + ROW_ONE
NODE_V, NODE_U, NODE_S = 0, 12, 16
COLS2 = NS
ZEROS = TABLE_ROWS * COLS2 // P


def after(eng, sem, value):
    if not isinstance(value, int) or value > 0:
        eng.wait_ge(sem, value)


def split_in_three(nc, then, x, rest, parts, done):
    then(nc.vector.tensor_copy(parts[0], x))
    then(nc.vector.tensor_tensor(rest, x, parts[0], ALU.subtract))
    then(nc.vector.tensor_copy(parts[1], rest))
    nc.vector.tensor_tensor(parts[2], rest, parts[1], ALU.subtract).then_inc(done, 1)


def prepare(nc, a, dram, keep):
    with ExitStack() as ctx:
        def sb(name, shape, dt):
            return ctx.enter_context(nc.sbuf_tensor(name, shape, dt))

        def sem(name):
            return ctx.enter_context(nc.semaphore(name))

        zero = keep["zero"]
        recv_i = sb("recv_i", [P, ALL_TILES], I32)
        part_i = sb("part_i", [P, ALL_TILES], I32)
        high = sb("high", [P, ALL_TILES], BF16)
        low = sb("low", [P, ALL_TILES], BF16)
        norm2 = sb("norm2", [P, ALL_TILES], F32)
        CHUNKS = 52
        CH = ALL_TILES // CHUNKS
        EDGE_HALF = ALL_TILES // 2
        square = sb("square", [P, 2, CH, XYZ], F32)
        x3 = sb("x3", [NODE_PARTS, NODE_COLS, 3, NS], BF16)
        xn = sb("xn", [NODE_PARTS, NODE_COLS, NS], F32)
        xc = sb("xc", [NODE_PARTS, NODE_COLS, NS], F32)
        xq = sb("xq", [NODE_PARTS, NODE_COLS, NS], F32)
        mean = sb("mean", [NODE_PARTS, NODE_COLS], F32)
        var = sb("var", [NODE_PARTS, NODE_COLS], F32)
        std = sb("std", [NODE_PARTS, NODE_COLS], F32)
        rstd = sb("rstd", [NODE_PARTS, NODE_COLS], F32)
        SP_COLS = ALL_TILES // SENDER_PARTS
        BASE_PARTS = 13
        BASE_COLS = STEPS // BASE_PARTS
        send_i = sb("send_i", [SENDER_PARTS, SP_COLS, P], I32)
        send_f = sb("send_f", [SENDER_PARTS, SP_COLS, P], F32)
        send_b = sb("send_b", [SENDER_PARTS, SP_COLS, P], BF16)
        tile_min = sb("tile_min", [SENDER_PARTS, SP_COLS], F32)
        step_min = sb("step_min", [BASE_PARTS, BASE_COLS, TILES], F32)
        base_f = sb("base_f", [BASE_PARTS, BASE_COLS], F32)
        base_i = sb("base_i", [BASE_PARTS, BASE_COLS], I32)
        base_by_tile = sb("base_by_tile", [BASE_PARTS, BASE_COLS, TILES], F32)
        tile_base = sb("tile_base", [SENDER_PARTS, SP_COLS], F32)
        farthest = sb("farthest", [SENDER_PARTS, 1], F32)
        farthest_row = sb("farthest_row", [1, SENDER_PARTS], F32)
        flag = sb("flag", [1, 1], F32)

        x_in, vec_in, recv_in, row_in = sem("x_in"), sem("vec_in"), sem("recv_in"), sem("row_in")
        const_in, zeroed, tables_out = sem("const_in"), sem("zeroed"), sem("tables_out")
        dve_step, split, rows_out = sem("dve_step"), sem("split"), sem("rows_out")
        var_done, std_done, x_done, x_out = sem("var_done"), sem("std_done"), sem("x_done"), sem("x_out")
        norm_done, length_done = sem("norm_done"), sem("length_done")
        send_in, min_done, min_moved = sem("send_in"), sem("min_done"), sem("min_moved")
        base_done, base_moved, place_done = sem("base_done"), sem("base_moved"), sem("place_done")
        sender_in, squared = sem("sender_in"), sem("squared")
        place_moved, base_in = sem("place_moved"), sem("base_in")

        with nc.Block() as block:
            @block.sync
            def _(sp):
                sp.dma_start(send_i[:], a["send_flat"]).then_inc(send_in, 16)
                sp.dma_start(xn[:], a["x"].rearrange("(p c) k -> p c k", p=NODE_PARTS)).then_inc(x_in, 16)
                sp.dma_start(recv_i[:], a["recv_flat"]).then_inc(row_in, 16)
                sp.wait_ge(base_in, 32)
                sp.dma_start(keep["unit"][:], a["vec"]).then_inc(vec_in, 16)
                for k in (1, 2):
                    for h in (0, HID):
                        sp.dma_start(keep[f"w1_{k}"][h:h + D, 0:D], a[f"w1_{k}"]).then_inc(const_in, 16)
                        sp.dma_start(keep[f"b1_{k}"][h:h + D, :], a[f"b1_{k}"]).then_inc(const_in, 16)
                        sp.dma_start(keep[f"w2_{k}"][h:h + D, :], a[f"w2_{k}"]).then_inc(const_in, 16)
                        sp.dma_start(keep[f"w2_{k}"][h + D:h + HK, :], a[f"b2_{k}"]).then_inc(const_in, 16)
                sp.dma_start(keep["by_part"][:], a["by_part"]).then_inc(const_in, 16)
                sp.wait_ge(zeroed, 1)
                for j in range(TABLES):
                    for h in range(2):
                        sp.dma_start(dram["sum1"][j].rearrange("(p r) k -> p (r k)", p=P)[
                            :, h * ZEROS:(h + 1) * ZEROS], zero[:]).then_inc(tables_out, 16)
                sp.wait_ge(split, 1)
                sp.dma_start(dram["recv_rows"][0].rearrange("(p t) -> p t", p=P), high[:]).then_inc(rows_out, 16)
                sp.dma_start(dram["recv_rows"][1].rearrange("(p t) -> p t", p=P), low[:]).then_inc(rows_out, 16)
                sp.dma_start(recv_i[:], a["recv_cols"]).then_inc(recv_in, 16)
                sp.dma_start(keep["sender"][:], a["send_cols"]).then_inc(sender_in, 16)
                sp.wait_ge(x_done, 1)
                sp.dma_start(dram["norm_x"].rearrange("(p c) k -> p c k", p=NODE_PARTS), xc[:]).then_inc(x_out, 16)
                sp.dma_start(dram["norm_x3"].rearrange("(p c) k -> p (c k)", p=NODE_PARTS),
                             x3[:].rearrange("p c h k -> p (c h k)")).then_inc(x_out, 16)
                sp.wait_ge(x_out, 32)
                sp.wait_ge(rows_out, 32)
                sp.wait_ge(place_moved, 32)
                sp.wait_ge(tables_out, 2 * 16 * TABLES)
                sp.wait_ge(const_in, 17 * 16)
                sp.wait_ge(sender_in, 16)

            @block.gpsimd
            def _(pool):
                nc.gpsimd.memset(zero[:], 0.0).then_inc(zeroed, 1)

            @block.scalar
            def _(act):
                act.wait_ge(min_done, 1)
                act.dma_start(dram["tile_min"][0:ALL_TILES].rearrange("(p t) -> p t", p=SENDER_PARTS),
                              tile_min[:]).then_inc(min_moved, 16)
                act.wait_ge(min_moved, 16)
                act.dma_start(step_min[:], dram["tile_min"][0:ALL_TILES].rearrange(
                    "(p s t) -> p s t", p=BASE_PARTS, t=TILES)).then_inc(min_moved, 16)
                act.wait_ge(base_done, 1)
                act.dma_start(dram["tile_base"][0:ALL_TILES].rearrange("(p s t) -> p s t", p=BASE_PARTS, t=TILES),
                              base_by_tile[:]).then_inc(base_moved, 16)
                act.dma_start(dram["base"][0:STEPS].rearrange("(p s) -> p s", p=BASE_PARTS),
                              base_i[:]).then_inc(base_moved, 16)
                act.wait_ge(base_moved, 32)
                act.dma_start(tile_base[:], dram["tile_base"][0:ALL_TILES].rearrange(
                    "(p t) -> p t", p=SENDER_PARTS)).then_inc(base_in, 16)
                act.dma_start(keep["base"][:], dram["base"][0:STEPS].rearrange("(o s) -> o s", o=1)).then_inc(base_in, 16)
                act.wait_ge(var_done, 1)
                nc.scalar.activation(std[:], var[:], ACT.Sqrt).then_inc(std_done, 1)
                act.wait_ge(place_done, 1)
                act.dma_start(dram["place_rows"][0].rearrange("(p t e) -> p t e", p=SENDER_PARTS, e=P),
                              send_b[:]).then_inc(place_moved, 16)
                act.dma_start(dram["farthest"][0:SENDER_PARTS].rearrange("(p o) -> p o", o=1),
                              farthest[:]).then_inc(place_moved, 16)
                act.wait_ge(vec_in, 16)
                for c in range(CHUNKS):
                    if c >= 2:
                        act.wait_ge(norm_done, c - 1)
                    nc.scalar.activation(square[:, c % 2, :, :], keep["unit"][:, c * CH:(c + 1) * CH, :],
                                         ACT.Square).then_inc(squared, 1)
                for h in range(2):
                    act.wait_ge(norm_done, (h + 1) * CHUNKS // 2)
                    length = norm2[:, h * EDGE_HALF:(h + 1) * EDGE_HALF]
                    nc.scalar.activation(length, length, ACT.Sqrt).then_inc(length_done, 1)
                act.wait_ge(place_moved, 32)
                act.dma_start(farthest_row[:], dram["farthest"][0:SENDER_PARTS].rearrange(
                    "(o p) -> o p", o=1)).then_inc(base_in, 16)

            @block.vector
            def _(dve):
                steps = [0]

                def then(ins):
                    steps[0] += 1
                    ins.then_inc(dve_step, 1)
                    dve.wait_ge(dve_step, steps[0])

                per_sender = [SENDER_PARTS, SP_COLS, P]
                dve.wait_ge(send_in, 16)
                then(nc.vector.tensor_copy(send_f[:], send_i[:]))
                nc.vector.tensor_reduce(tile_min[:], send_f[:], AX_X, ALU.min).then_inc(min_done, 1)

                per_node = [NODE_PARTS, NODE_COLS, NS]
                dve.wait_ge(x_in, 16)
                then(nc.vector.reduce_sum(mean[:], xn[:], AX_X))
                then(nc.vector.tensor_scalar(mean[:], mean[:], 1.0 / NS, None, ALU.mult))
                then(nc.vector.tensor_tensor(xc[:], xn[:], mean[:].unsqueeze(2).to_broadcast(per_node), ALU.subtract))

                dve.wait_ge(min_moved, 32)
                then(nc.vector.tensor_reduce(base_f[:], step_min[:], AX_X, ALU.min))
                then(nc.vector.tensor_scalar(base_f[:], base_f[:], float(N - WINDOW), None, ALU.min))
                then(nc.vector.tensor_copy(base_i[:], base_f[:]))
                nc.vector.tensor_copy(base_by_tile[:], base_f[:].unsqueeze(2).to_broadcast(
                    [BASE_PARTS, BASE_COLS, TILES])).then_inc(base_done, 1)

                then(nc.vector.tensor_tensor(xq[:], xc[:], xc[:], ALU.mult))
                then(nc.vector.reduce_sum(var[:], xq[:], AX_X))
                nc.vector.tensor_scalar(var[:], var[:], 1.0 / NS, EPS, ALU.mult, ALU.add).then_inc(var_done, 1)

                dve.wait_ge(row_in, 16)
                then(nc.vector.tensor_scalar(part_i[:], recv_i[:], 7, None, ALU.logical_shift_right))
                then(nc.vector.tensor_copy(high[:], part_i[:]))
                then(nc.vector.tensor_scalar(part_i[:], recv_i[:], 127, None, ALU.bitwise_and))
                nc.vector.tensor_copy(low[:], part_i[:]).then_inc(split, 1)

                dve.wait_ge(std_done, 1)
                then(nc.vector.reciprocal(rstd[:], std[:]))
                then(nc.vector.tensor_tensor(xc[:], xc[:], rstd[:].unsqueeze(2).to_broadcast(per_node), ALU.mult))
                then(nc.vector.tensor_scalar(xc[:], xc[:], 0.0, None, ALU.max))
                split_in_three(nc, then, xc[:], xq[:], [x3[:, :, h, :] for h in range(3)], x_done)

                dve.wait_ge(base_in, 32)
                then(nc.vector.tensor_tensor(send_f[:], send_f[:], tile_base[:].unsqueeze(2).to_broadcast(per_sender),
                                             ALU.subtract))
                then(nc.vector.tensor_copy(send_b[:], send_f[:]))
                nc.vector.tensor_reduce(farthest[:], send_f[:].rearrange("p t e -> p (t e)"), AX_X,
                                        ALU.max).then_inc(place_done, 1)

                for c in range(CHUNKS):
                    dve.wait_ge(squared, c + 1)
                    nc.vector.reduce_sum(norm2[:, c * CH:(c + 1) * CH], square[:, c % 2, :, :], AX_X).then_inc(norm_done, 1)
                for h in range(2):
                    half = slice(h * EDGE_HALF, (h + 1) * EDGE_HALF)
                    unit, length = keep["unit"][:, half, :], norm2[:, half]
                    dve.wait_ge(length_done, h + 1)
                    then(nc.vector.tensor_scalar(length, length, 1e-12, None, ALU.add))
                    then(nc.vector.reciprocal(length, length))
                    then(nc.vector.scalar_tensor_tensor(
                        out=unit, in0=unit, scalar=float(np.sqrt(3.0)),
                        in1=length.unsqueeze(2).to_broadcast([P, EDGE_HALF, XYZ]), op0=ALU.mult, op1=ALU.mult))

                dve.wait_ge(const_in, 17 * 16)
                dve.wait_ge(recv_in, 16)
                then(nc.vector.tensor_copy(keep["recv"][:], recv_i[:]))
                then(nc.vector.tensor_scalar(keep["target"][:].bitcast(F32), keep["recv"][:], -1.0,
                                             keep["by_part"][:, 2:3], ALU.mult, ALU.add))

                dve.wait_ge(base_in, 48)
                then(nc.vector.tensor_reduce(flag[:], farthest_row[:], AX_X, ALU.max))
                then(nc.vector.tensor_scalar(flag[:], flag[:], float(WINDOW - 1), None, ALU.is_le))
                then(nc.vector.tensor_copy(keep["in_windows"][:], flag[:]))


def constants(nc, keep):
    filled = nc.semaphore("filled")
    with filled as filled, nc.Block() as block:
        @block.vector
        def _(dve):
            for k in (1, 2):
                nc.vector.memset(keep[f"w1_{k}"][:], 0.0).then_inc(filled, 1)
                nc.vector.memset(keep[f"b1_{k}"][:], 1.0).then_inc(filled, 1)
                nc.vector.memset(keep[f"w2_{k}"][:], 0.0).then_inc(filled, 1)
            nc.vector.memset(keep["halves"][:], 1.0).then_inc(filled, 1)
            dve.wait_ge(filled, 7)
            nc.vector.memset(keep["halves"][0:1, :], float(P)).then_inc(filled, 1)
            dve.wait_ge(filled, 8)


def edge_layer(nc, a, dram, keep, layer):
    first = layer == 1
    COLS = FIRST + 1 if first else COLS2
    IN, OUT = (NS, NV + NS) if first else (NV + NS, NS)
    table = dram["norm_x"] if first else dram["node"]
    table3 = dram["norm_x3"] if first else dram["node3"]
    GW = NS if first else ROW
    sums = dram["sum1"] if first else dram["sum2"]
    SW = ROW if first else COLS2
    w1, b1, w2 = (keep[f"{n}_{layer}"] for n in ("w1", "b1", "w2"))
    unit, recv, sender, target = keep["unit"], keep["recv"], keep["sender"], keep["target"]

    with ExitStack() as ctx:
        def sb(name, shape, dt):
            return ctx.enter_context(nc.sbuf_tensor(f"{name}_{layer}", shape, dt))

        def pb(name):
            return ctx.enter_context(nc.psum_tensor(f"{name}_{layer}", [P, 512], F32))

        def sem(name):
            return ctx.enter_context(nc.semaphore(f"{name}_{layer}"))

        def two(name):
            return [sem(f"{name}_even"), sem(f"{name}_odd")]

        attr = sb("attr", [P, 2, HALF], F32)
        recv_row = sb("recv_row", [2, 2, STEP], BF16)
        hidden = sb("hidden", [P, 2, HALF], F32)
        hidden_rest = sb("hidden_rest", [P, HALF], F32)
        hidden_parts = sb("hidden_parts", [P, 2, 3, HALF], BF16)
        stacked = sb("stacked", [P, 2, 2, 2, HALF], BF16)
        w2_parts = sb("w2_parts", [P, 4, WN], BF16)
        w2_rest = sb("w2_rest", [P, WN], F32)
        send_idx = sb("send_idx", [P, 2, TILES], U32)
        target_idx = sb("target_idx", [P, 2, TILES], U32)
        node = sb("node", [P, 2, TILES, GW], F32)
        prod = sb("prod", [P, 2, 2, WN], F32)
        SUMMED = MSG_S if first else 0
        same = sb("same", [P, 2, STEP], F32)
        apart = sb("apart", [P, 2, GROUP * P], BF16)
        message = sb("message", [P, 2, TILES, SUMMED + COLS], F32)
        summed = sb("summed", [P, 2, TILES, COLS], F32)
        rows = sb("rows", [P, 2, TILES, SW], F32)
        vdot = sb("vdot", [P, TILES, NV, XYZ], F32)
        shift = sb("shift", [P, TILES], F32)
        window = sb("window", [WINDOW, 2, 3 * GW], BF16)
        place_row = sb("place_row", [P, 2, STEP], BF16)
        at_place = sb("at_place", [WINDOW, 2, STEP], BF16)

        hid_ps = pb("hid_ps")
        weight_ps = ctx.enter_context(nc.psum_tensor(f"weight_ps_{layer}", [P, 2, 2, 512], F32))
        recv_ps = pb("recv_ps")
        comb_ps = pb("comb_ps")
        comb = comb_ps[:, 0:TILES * COLS].rearrange("p (t k) -> p t k", k=COLS)
        node_ps = comb_ps[:, TILES * COLS:TILES * (COLS + GW)].rearrange("p (t k) -> p t k", k=GW)

        next_zeroed = sem("next_zeroed")
        gate = sem("gate")
        attr_in = two("attr_in")
        recv_in = two("recv_in")
        stacked_in = two("stacked_in")
        window_in = two("window_in")
        placed = sem("placed")
        picked = sem("picked")
        node_ready = sem("node_ready")
        gathered = two("gathered")
        scattered = [sem(f"scattered{j}") for j in range(TABLES)]
        rows_free = sem("rows_free")
        send_staged = sem("send_staged")
        hid_done = sem("hid_done")
        hidden_ready = sem("hidden_ready")
        hidden_high = sem("hidden_high")
        hidden_less = sem("hidden_less")
        hidden_middle = sem("hidden_middle")
        hidden_low = sem("hidden_low")
        w2_split = sem("w2_split")
        weights_ready = sem("weights_ready")
        weights_used = sem("weights_used")
        reduced = sem("reduced")
        recv_ready = sem("recv_ready")
        apart_done = sem("apart_done")
        same_done = sem("same_done")
        message_set = sem("message_set")
        summed_ready = sem("summed_ready")
        vdot_done = sem("vdot_done")
        vectors_done = sem("vectors_done")
        comb_done = sem("comb_done")
        rows_ready = sem("rows_ready")
        shift_done = sem("shift_done")
        target_done = sem("target_done")

        class Step:

            def __init__(self, half, odd):
                self.half, self.odd = half, odd
                self.n = half * 2 + odd

            def next(self):
                return Step(self.half, 1) if self.odd == 0 else Step(self.half + 1, 0)

            def prev(self):
                return Step(self.half, 0) if self.odd == 1 else Step(self.half - 1, 1)

            @property
            def has_prev(self):
                return not isinstance(self.n, int) or self.n > 0

            @property
            def has_next(self):
                return not isinstance(self.n, int) or self.n < STEPS - 1

            def cols(self, of, start=0, width=TILES):
                return of[:, bass.ds(self.n * TILES + start, width)]

        def every_step(eng, body, alone=3):
            for n in range(alone):
                body(Step(n // 2, n % 2))
            with eng.Fori(alone // 2, STEPS // 2 - 1) as half:
                body(Step(half, 1))
                body(Step(half + 1, 0))
            for n in (STEPS - 2, STEPS - 1):
                body(Step(n // 2, n % 2))

        def both_ways(eng, program):
            flag = eng.value_load(keep["in_windows"][0:1, 0:1], min_val=0, max_val=1)
            with eng.If(flag):
                program(True)
            with eng.Else():
                program(False)

        with nc.Block() as block:
            @block.sync
            def _(sp):
                def program(in_windows):
                    def load_attributes(s):
                        after(sp, hid_done, s.n - 1)
                        sp.sem_inc(gate, 1)
                        for h in range(2):
                            sp.dma_start(attr[HID * h:HID * h + D, s.odd, :],
                                         a["attr"][h][:, bass.ds(s.n * HALF, HALF)]).then_inc(attr_in[s.odd], 16)

                    def load_rows(s):
                        after(sp, recv_ready, (s.n - 1) * (TILES // GROUP))
                        sp.sem_inc(gate, 1)
                        sp.dma_start(recv_row[:, s.odd, :],
                                     dram["recv_rows"][:, bass.ds(s.n * STEP, STEP)]).then_inc(recv_in[s.odd], 16)
                        if in_windows:
                            after(sp, picked, s.n - 1)
                            after(sp, placed, s.n - 1)
                            sp.sem_inc(gate, 1)
                            base = sp.value_load(keep["base"][0:1, bass.ds(s.n, 1)], min_val=0, max_val=N - WINDOW)
                            sp.dma_start(window[:, s.odd, :],
                                         table3[bass.ds(base, WINDOW), :]).then_inc(window_in[s.odd], 16)
                            sp.dma_start(place_row[:, s.odd, :], dram["place_rows"][:, bass.ds(s.n * STEP, STEP)]
                                         .to_broadcast([P, STEP])).then_inc(window_in[s.odd], 16)

                    def stack(s):
                        after(sp, hidden_low, s.n + 1)
                        sp.sem_inc(gate, 1)
                        after(sp, weights_ready, PAIRS * (s.n - 1))
                        sp.sem_inc(gate, 1)
                        for h in range(2):
                            here, there = slice(HID * h, HID * h + HID), slice(HID - HID * h, P - HID * h)
                            sp.dma_start(stacked[here, s.odd, h, :, :], hidden_parts[here, s.odd, 0:1, :]
                                         .to_broadcast([HID, 2, HALF])).then_inc(stacked_in[s.odd], 16)
                            sp.dma_start(stacked[there, s.odd, h, :, :],
                                         hidden_parts[here, s.odd, 1:3, :]).then_inc(stacked_in[s.odd], 16)

                    def body(s):
                        if first and isinstance(s.n, int) and s.n < TABLES:
                            sp.dma_start(dram["sum2"][s.n].rearrange("(p r) k -> p (r k)", p=P),
                                         keep["zero"][:]).then_inc(next_zeroed, 16)
                        if s.has_next and s.next().has_next:
                            load_attributes(s.next().next())
                        if s.has_next:
                            load_rows(s.next())
                            stack(s.next())

                    load_attributes(Step(0, 0))
                    load_attributes(Step(0, 1))
                    load_rows(Step(0, 0))
                    stack(Step(0, 0))
                    every_step(sp, body, alone=TABLES + 1 if first else 3)
                    if first:
                        sp.wait_ge(next_zeroed, TABLES * 16)

                both_ways(sp, program)

            @block.gpsimd
            def _(pool):
                def program(in_windows):
                    def gather(s):
                        after(pool, send_staged, s.n + 1)
                        after(pool, weights_used, PAIRS * (s.n - 1))
                        pool.sem_inc(gate, 1)
                        for j in range(TILES):
                            nc.gpsimd.indirect_dma_start(
                                node[:, s.odd, j, :], None, table[:, :],
                                bass.IndirectOffsetOnAxis(send_idx[:, s.odd, j:j + 1], 0),
                            ).then_inc(gathered[s.odd], 16)

                    def scatter(s):
                        after(pool, rows_ready, 2 * (s.n + 1))
                        for j in range(TABLES):
                            if j < ASK_ALL:
                                after(pool, scattered[j], s.n * 16)
                                pool.sem_inc(gate, 1)
                            elif j == ASK_ALL:
                                for later in range(j, TABLES):
                                    after(pool, scattered[later], s.n * 16)
                                pool.sem_inc(rows_free, 1)
                            nc.gpsimd.indirect_dma_start(
                                sums[j][:, :], bass.IndirectOffsetOnAxis(target_idx[:, s.odd, j:j + 1], 0),
                                rows[:, s.odd, j, :], None, compute_op=ALU.add,
                            ).then_inc(scattered[j], 16)

                    def body(s):
                        if s.has_next and not in_windows:
                            gather(s.next())
                        if s.has_prev and s.prev().has_prev:
                            scatter(s.prev().prev())

                    if not in_windows:
                        gather(Step(0, 0))
                    every_step(pool, body)
                    scatter(Step(STEPS // 2 - 1, 1))
                    scatter(Step(STEPS // 2, 0))
                    for j in range(TABLES):
                        pool.wait_ge(scattered[j], STEPS * 16)

                both_ways(pool, program)

            @block.scalar
            def _(act):
                def program(in_windows):
                    def stage_sender(s):
                        after(act, gathered[s.odd], s.half * TILES * 16)
                        nc.scalar.copy(send_idx[:, s.odd, :], s.cols(sender)).then_inc(send_staged, 1)

                    def move_nodes(s):
                        after(act, picked, s.n + 1)
                        after(act, comb_done, s.n - 1)
                        after(act, weights_used, PAIRS * (s.n - 1))
                        nc.scalar.copy(node[:, s.odd, :, :], node_ps).then_inc(node_ready, 1)

                    def relu(s):
                        after(act, hid_done, s.n + 1)
                        after(act, hidden_less, s.n - 1)
                        nc.scalar.activation(hidden[:, s.odd, :], hid_ps[:, :], ACT.Relu,
                                             bias=b1[:, :]).then_inc(hidden_ready, 1)

                    def hidden_high_part(s):
                        after(act, hidden_ready, s.n + 1)
                        after(act, stacked_in[s.odd], s.half * 4 * 16)
                        nc.scalar.copy(hidden_parts[:, s.odd, 0, :], hidden[:, s.odd, :]).then_inc(hidden_high, 1)

                    def hidden_middle_part(s):
                        after(act, hidden_less, s.n + 1)
                        nc.scalar.copy(hidden_parts[:, s.odd, 1, :], hidden_rest[:]).then_inc(hidden_middle, 1)

                    def equal_receivers(s, c):
                        after(act, recv_ready, 2 * s.n + c + 1)
                        after(act, same_done, 2 * s.n + c - 1)
                        for t in range(GROUP):
                            nc.scalar.activation(
                                apart[:, c, t * P:(t + 1) * P], recv_ps[:, t * P:(t + 1) * P], ACT.Square,
                                bias=s.cols(recv, c * GROUP + t, 1), scale=-1.0).then_inc(apart_done, 1)
                        after(act, apart_done, GROUP * (2 * s.n + c + 1))
                        after(act, comb_done, s.n - 1)
                        nc.scalar.activation(same[:, s.odd, c * GROUP * P:(c + 1) * GROUP * P], apart[:, c, :],
                                             ACT.Relu, bias=1.0, scale=-1.0).then_inc(same_done, 1)

                    def move_sums(s):
                        after(act, rows_ready, 2 * (s.n - 1))
                        after(act, comb_done, s.n + 1)
                        nc.scalar.copy(summed[:, s.odd, :, :], comb).then_inc(summed_ready, 1)

                    def stage_rows(s):
                        after(act, rows_free, s.n)
                        after(act, summed_ready, s.n + 1)
                        nc.scalar.copy(rows[:, s.odd, :, :], summed[:, s.odd, :, 0:SW]).then_inc(rows_ready, 1)
                        if first:
                            after(act, target_done, s.n + 1)
                        nc.scalar.copy(target_idx[:, s.odd, :], s.cols(target)).then_inc(rows_ready, 1)

                    def body(s):
                        if s.has_next and not in_windows:
                            stage_sender(s.next())
                        equal_receivers(s, 0)
                        if s.has_prev and s.prev().has_prev:
                            stage_rows(s.prev().prev())
                        if s.has_next and s.next().has_next:
                            relu(s.next().next())
                            hidden_high_part(s.next().next())
                        equal_receivers(s, 1)
                        if s.has_next and in_windows:
                            move_nodes(s.next())
                        if s.has_next and s.next().has_next:
                            hidden_middle_part(s.next().next())
                        if s.has_prev:
                            move_sums(s.prev())

                    for s in (Step(0, 0), Step(0, 1)):
                        relu(s)
                        hidden_high_part(s)
                        hidden_middle_part(s)
                    if in_windows:
                        move_nodes(Step(0, 0))
                    else:
                        stage_sender(Step(0, 0))
                    every_step(act, body)
                    last = Step(STEPS // 2, 0)
                    stage_rows(last.prev())
                    move_sums(last)
                    stage_rows(last)

                both_ways(act, program)

            @block.tensor
            def _(pe):
                def program(in_windows):
                    def hidden_product(s):
                        after(pe, attr_in[s.odd], (s.half + 1) * 2 * 16)
                        after(pe, hidden_ready, s.n)
                        pe.sem_inc(gate, 1)
                        for h in range(2):
                            lo = HID * h
                            mm = nc.tensor.matmul(hid_ps[lo:lo + HID, :], w1[lo:lo + D, :],
                                                  attr[lo:lo + D, s.odd, :], start=True, stop=True)
                        mm.then_inc(hid_done, 1)

                    def weight_product(s, j):
                        if j == 0:
                            after(pe, stacked_in[s.odd], (s.half + 1) * 4 * 16)
                        after(pe, weights_used, PAIRS * s.n + j - 1)
                        pe.sem_inc(gate, 1)
                        for h in range(2):
                            for n, (x, w) in enumerate(((0, 0), (0, 1), (1, 2 + h))):
                                mm = nc.tensor.matmul(weight_ps[:, j % 2, h, 0:WN],
                                                      stacked[:, s.odd, h, x, j * P:(j + 1) * P],
                                                      w2_parts[:, w, :], start=(n == 0), stop=(n == 2))
                        mm.then_inc(weights_ready, 1)

                    def pick_nodes(s):
                        after(pe, placed, s.n + 1)
                        after(pe, window_in[s.odd], (s.half + 1) * 2 * 16)
                        after(pe, node_ready, s.n)
                        after(pe, summed_ready, s.n - 2)
                        for t in range(TILES):
                            for h in range(3):
                                mm = nc.tensor.matmul(node_ps[:, t, :], at_place[:, s.odd, t * P:(t + 1) * P],
                                                      window[:, s.odd, h * GW:(h + 1) * GW],
                                                      start=(h == 0), stop=(h == 2))
                        mm.then_inc(picked, 1)

                    def receivers(s, c):
                        after(pe, recv_in[s.odd], (s.half + 1) * 16)
                        after(pe, apart_done, GROUP * (2 * s.n + c))
                        nc.tensor.matmul(recv_ps[:, :], keep["halves"][:, :],
                                         recv_row[:, s.odd, c * GROUP * P:(c + 1) * GROUP * P],
                                         start=True, stop=True).then_inc(recv_ready, 1)

                    def combine_messages(s):
                        after(pe, same_done, 2 * s.n + 2)
                        after(pe, *((vectors_done, s.n + 1) if first else (reduced, PAIRS * (s.n + 1))))
                        after(pe, summed_ready, s.n)
                        for t in range(TILES):
                            mm = nc.tensor.matmul(comb[:, t, :], same[:, s.odd, t * P:(t + 1) * P],
                                                  message[:, s.odd, t, SUMMED:SUMMED + COLS], start=True, stop=True)
                        mm.then_inc(comb_done, 1)

                    def body(s):
                        weight_product(s, 0)
                        receivers(s, 0)
                        weight_product(s, 1)
                        if s.has_next and s.next().has_next:
                            hidden_product(s.next().next())
                        receivers(s, 1)
                        weight_product(s, 2)
                        weight_product(s, 3)
                        if s.has_next and in_windows:
                            pick_nodes(s.next())
                        if s.has_prev:
                            combine_messages(s.prev())

                    for s in (Step(0, 0), Step(0, 1)):
                        hidden_product(s)
                    if in_windows:
                        pick_nodes(Step(0, 0))
                    pe.wait_ge(w2_split, 7)
                    if first:
                        pe.wait_ge(message_set, 3)
                    every_step(pe, body)
                    combine_messages(Step(STEPS // 2, 0))

                both_ways(pe, program)

            @block.vector
            def _(dve):
                def split_w2():
                    lower, upper = slice(0, HID), slice(HID, P)
                    nc.vector.tensor_copy(w2_parts[:, 0, :], w2[:]).then_inc(w2_split, 1)
                    dve.wait_ge(w2_split, 1)
                    nc.vector.tensor_tensor(w2_rest[:], w2[:], w2_parts[:, 0, :], ALU.subtract).then_inc(w2_split, 1)
                    dve.wait_ge(w2_split, 2)
                    nc.vector.tensor_copy(w2_parts[:, 1, :], w2_rest[:]).then_inc(w2_split, 1)
                    dve.wait_ge(w2_split, 3)
                    for low, high, n in ((lower, upper, 2), (upper, lower, 3)):
                        nc.vector.tensor_tensor(w2_parts[low, n, :], w2_rest[low, :], w2_parts[low, 1, :],
                                                ALU.subtract).then_inc(w2_split, 1)
                        nc.vector.tensor_copy(w2_parts[high, n, :], w2_parts[high, 0, :]).then_inc(w2_split, 1)

                def set_messages():
                    nc.vector.memset(message[:], 0.0).then_inc(message_set, 1)
                    dve.wait_ge(message_set, 1)
                    nc.vector.memset(message[:, :, :, SUMMED + ROW_ONE], 1.0).then_inc(message_set, 1)
                    nc.vector.tensor_copy(message[:, :, :, SUMMED + FIRST], keep["by_part"][:, 0:1].unsqueeze(2)
                                          .to_broadcast([P, 2, TILES])).then_inc(message_set, 1)
                    dve.wait_ge(message_set, 3)

                def program(in_windows):
                    def node_wait(s):
                        if in_windows:
                            dve.wait_ge(node_ready, s.n + 1)
                        else:
                            dve.wait_ge(gathered[s.odd], (s.half + 1) * TILES * 16)

                    def hidden_rest_part(s):
                        dve.wait_ge(hidden_high, s.n + 1)
                        after(dve, hidden_low, s.n)
                        nc.vector.tensor_tensor(hidden_rest[:], hidden[:, s.odd, :], hidden_parts[:, s.odd, 0, :],
                                                ALU.subtract).then_inc(hidden_less, 1)

                    def hidden_low_part(s):
                        dve.wait_ge(hidden_middle, s.n + 1)
                        nc.vector.tensor_tensor(hidden_parts[:, s.odd, 2, :], hidden_rest[:],
                                                hidden_parts[:, s.odd, 1, :], ALU.subtract).then_inc(hidden_low, 1)

                    def vector_products(s):
                        node_wait(s)
                        after(dve, vectors_done, s.n)
                        nc.vector.tensor_tensor(
                            vdot[:], node[:, s.odd, :, NODE_V:NODE_V + NV * XYZ].rearrange("p t (j c) -> p t j c", c=XYZ),
                            s.cols(unit).unsqueeze(2).to_broadcast([P, TILES, NV, XYZ]),
                            ALU.mult).then_inc(vdot_done, 1)

                    def vector_inputs(s):
                        dve.wait_ge(vdot_done, s.n + 1)
                        nc.vector.reduce_sum(node[:, s.odd, :, NODE_U:NODE_U + NV], vdot[:], AX_X).then_inc(vectors_done, 1)

                    def product(s, j):
                        if j == 0 and first:
                            node_wait(s)
                        elif j == 0:
                            dve.wait_ge(vectors_done, s.n + 1)
                        dve.wait_ge(weights_ready, PAIRS * s.n + j + 1)
                        after(dve, reduced, PAIRS * s.n + j - 1)
                        w = weight_ps[:, j % 2, :, 0:WN].rearrange("p h (i o) -> p h i o", o=OUT)
                        x = node[:, s.odd, :, GW - IN:GW].rearrange("p (h j) i -> p h j i", h=2)[:, :, j, :]
                        nc.vector.tensor_tensor(
                            prod[:, j % 2, :, :].rearrange("p h (i o) -> p h i o", o=OUT), w,
                            x.unsqueeze(3).to_broadcast([P, 2, IN, OUT]), ALU.mult).then_inc(weights_used, 1)

                    def reduce(s, j):
                        dve.wait_ge(weights_used, PAIRS * s.n + j + 1)
                        after(dve, comb_done, s.n - 1)
                        out = message[:, s.odd, :, 0:OUT].rearrange("p (h j) o -> p h j o", h=2)[:, :, j, :]
                        nc.vector.reduce_sum(out, prod[:, j % 2, :, :].rearrange("p h (i o) -> p h o i", o=OUT),
                                             AX_X).then_inc(reduced, 1)

                    def place(s):
                        dve.wait_ge(window_in[s.odd], (s.half + 1) * 2 * 16)
                        after(dve, picked, s.n - 1)
                        nc.vector.tensor_scalar(at_place[:, s.odd, :], place_row[:, s.odd, :],
                                                keep["by_part"][:, 3:4], None, ALU.is_equal).then_inc(placed, 1)

                    def vector_messages(s):
                        dve.wait_ge(reduced, PAIRS * (s.n + 1))
                        nc.vector.tensor_tensor(
                            message[:, s.odd, :, MSG_V:MSG_V_END].rearrange("p t (j c) -> p t j c", c=XYZ),
                            message[:, s.odd, :, MSG_T:MSG_T + NV].unsqueeze(3).to_broadcast([P, TILES, NV, XYZ]),
                            s.cols(unit).unsqueeze(2).to_broadcast([P, TILES, NV, XYZ]),
                            ALU.mult).then_inc(vectors_done, 1)

                    def first_of_receiver(s):
                        dve.wait_ge(summed_ready, s.n + 1)
                        after(dve, target_done, s.n)
                        nc.vector.scalar_tensor_tensor(out=shift[:], in0=summed[:, s.odd, :, FIRST],
                                                       scalar=keep["by_part"][:, 1:2], in1=s.cols(target.bitcast(F32)),
                                                       op0=ALU.is_gt, op1=ALU.mult).then_inc(shift_done, 1)

                    def targets(s):
                        dve.wait_ge(shift_done, s.n + 1)
                        nc.vector.tensor_tensor(s.cols(target), s.cols(recv), shift[:], ALU.add).then_inc(target_done, 1)

                    def body(s):
                        product(s, 0)
                        if first and s.has_prev:
                            vector_messages(s.prev())
                            if s.prev().has_prev:
                                first_of_receiver(s.prev().prev())
                        product(s, 1)
                        if first and s.has_prev and s.prev().has_prev:
                            targets(s.prev().prev())
                        reduce(s, 0)
                        if s.has_next and in_windows:
                            place(s.next())
                        product(s, 2)
                        reduce(s, 1)
                        if s.has_next and s.next().has_next:
                            hidden_rest_part(s.next().next())
                        product(s, 3)
                        reduce(s, 2)
                        if s.has_next and not first:
                            vector_products(s.next())
                        if s.has_next and s.next().has_next:
                            hidden_low_part(s.next().next())
                        if s.has_next and not first:
                            vector_inputs(s.next())
                        reduce(s, 3)

                    for s in (Step(0, 0), Step(0, 1)):
                        hidden_rest_part(s)
                        hidden_low_part(s)
                    if in_windows:
                        place(Step(0, 0))
                    if not first:
                        vector_products(Step(0, 0))
                        vector_inputs(Step(0, 0))
                    every_step(dve, body)
                    last = Step(STEPS // 2, 0)
                    if first:
                        vector_messages(last)
                        for s in (last.prev(), last):
                            first_of_receiver(s)
                            targets(s)

                split_w2()
                if first:
                    set_messages()
                both_ways(dve, program)


def node_layer(nc, a, dram, keep, layer, out):
    first = layer == 1
    sums, W = (dram["sum1"], ROW) if first else (dram["sum2"], COLS2)
    SCALE = 1.0 / np.sqrt(NS) if first else 1.0 / np.sqrt(NS + NV)
    S_AT = ROW_S if first else 0
    BUFS = 3
    PN, CN = NODE_PARTS, NODE_COLS
    with ExitStack() as ctx:
        def sb(name, shape, dt=F32):
            return ctx.enter_context(nc.sbuf_tensor(f"{name}_n{layer}", shape, dt))

        def sem(name):
            return ctx.enter_context(nc.semaphore(f"{name}_n{layer}"))

        total = sb("total", [PN, CN, W])
        part = sb("part", [PN, BUFS, CN * W])
        square = sb("square", [PN, CN, NS])
        ones = sb("ones", [PN, P])
        gain, bias = sb("gain", [PN, NS]), sb("bias", [PN, NS])
        vgain = sb("vgain", [PN, NV])
        colsum = sb("colsum", [PN, NS])
        mean = sb("mean", [PN, NS])
        var = sb("var", [PN, NS])
        std = sb("std", [PN, NS])
        result = sb("result", [PN, CN, ROW if first else NS])
        result3 = sb("result3", [PN, CN, 3, ROW if first else 1], BF16)
        rest = sb("rest", [PN, CN, ROW if first else 1])
        x_old = sb("x_old", [PN, CN, NS])
        stat_ps = ctx.enter_context(nc.psum_tensor(f"stat_ps_n{layer}", [P, 512], F32))
        table_in = [sem(f"table_in{b}") for b in range(BUFS)]
        total_in, par_in, ones_done, x_in = sem("total_in"), sem("par_in"), sem("ones_done"), sem("x_in")
        added, step, colsum_done, stat_done = sem("added"), sem("step"), sem("colsum_done"), sem("stat_done")
        var_done, std_done, result_done, result_out = (
            sem("var_done"), sem("std_done"), sem("result_done"), sem("result_out"))
        STATS = 3 if first else 2

        with nc.Block() as block:
            @block.sync
            def _(sp):
                def table_of(j):
                    return sums[j][0:N, :].rearrange("(p c) k -> p (c k)", p=PN)

                def row_of(v, n):
                    return v.rearrange("(o k) -> o k", o=1).to_broadcast([PN, n])

                sp.dma_start(total[:].rearrange("p c k -> p (c k)"), table_of(0)).then_inc(total_in, 16)
                for j in range(1, TABLES):
                    after(sp, added, j - BUFS)
                    sp.dma_start(part[:, j % BUFS, :], table_of(j)).then_inc(table_in[j % BUFS], 16)
                sp.dma_start(gain[:], row_of(a[f"gs_{layer}"], NS)).then_inc(par_in, 16)
                sp.dma_start(bias[:], row_of(a[f"bs_{layer}"], NS)).then_inc(par_in, 16)
                if first:
                    sp.dma_start(vgain[:], row_of(a["gv_1"], NV)).then_inc(par_in, 16)
                else:
                    sp.dma_start(x_old[:], a["x"].rearrange("(p c) k -> p c k", p=PN)).then_inc(x_in, 16)
                sp.wait_ge(result_done, 1)
                sp.dma_start(out.rearrange("(p c) k -> p c k", p=PN), result[:]).then_inc(result_out, 16)
                if first:
                    sp.dma_start(dram["node3"].rearrange("(p c) k -> p (c k)", p=PN),
                                 result3[:].rearrange("p c h k -> p (c h k)")).then_inc(result_out, 16)
                sp.wait_ge(result_out, 32 if first else 16)

            @block.gpsimd
            def _(pool):
                nc.gpsimd.memset(ones[:], 1.0).then_inc(ones_done, 1)

            @block.tensor
            def _(pe):
                pe.wait_ge(ones_done, 1)
                for n in range(STATS):
                    k = NS if n < 2 else NV
                    pe.wait_ge(colsum_done, n + 1)
                    nc.tensor.matmul(stat_ps[0:PN, n * NS:n * NS + k], ones[:, 0:PN], colsum[:, 0:k],
                                     start=True, stop=True).then_inc(stat_done, 1)

            @block.scalar
            def _(act):
                for n in range(STATS - 1):
                    k = NS if n < 1 else NV
                    act.wait_ge(var_done, n + 1)
                    nc.scalar.activation(std[:, 0:k], var[:, 0:k], ACT.Sqrt).then_inc(std_done, 1)

            @block.vector
            def _(dve):
                steps = [0]

                def then(ins):
                    steps[0] += 1
                    ins.then_inc(step, 1)
                    dve.wait_ge(step, steps[0])

                def over_nodes(v, k):
                    return v[:, 0:k].unsqueeze(1).to_broadcast([PN, CN, k])

                flat = total[:].rearrange("p c k -> p (c k)")
                dve.wait_ge(total_in, 16)
                for j in range(1, TABLES):
                    dve.wait_ge(table_in[j % BUFS], 16 * ((j - (j % BUFS or BUFS)) // BUFS + 1))
                    nc.vector.tensor_tensor(flat, flat, part[:, j % BUFS, :], ALU.add).then_inc(added, 1)
                    dve.wait_ge(added, j)
                per_count = keep["per_count"]
                if first:
                    then(nc.vector.tensor_scalar(per_count[:], total[:, :, ROW_ONE], 1.0, None, ALU.max))
                    then(nc.vector.reciprocal(per_count[:], per_count[:]))
                then(nc.vector.scalar_tensor_tensor(
                    out=total[:], in0=total[:], scalar=float(SCALE),
                    in1=per_count[:].unsqueeze(2).to_broadcast([PN, CN, W]), op0=ALU.mult, op1=ALU.mult))
                s = total[:, :, S_AT:S_AT + NS]
                nc.vector.reduce_sum(colsum[:], s.rearrange("p c k -> p k c"), AX_X).then_inc(colsum_done, 1)
                dve.wait_ge(stat_done, 1)
                then(nc.vector.tensor_scalar(mean[:], stat_ps[0:PN, 0:NS], 1.0 / N, None, ALU.mult))
                then(nc.vector.tensor_tensor(s, s, over_nodes(mean, NS), ALU.subtract))
                then(nc.vector.tensor_tensor(square[:], s, s, ALU.mult))
                nc.vector.reduce_sum(colsum[:], square[:].rearrange("p c k -> p k c"), AX_X).then_inc(colsum_done, 1)
                dve.wait_ge(stat_done, 2)
                nc.vector.tensor_scalar(var[:], stat_ps[0:PN, NS:2 * NS], 1.0 / N, EPS,
                                        ALU.mult, ALU.add).then_inc(var_done, 1)
                dve.wait_ge(std_done, 1)
                dve.wait_ge(par_in, 48 if first else 32)
                then(nc.vector.reciprocal(mean[:], std[:]))
                then(nc.vector.tensor_tensor(gain[:], gain[:], mean[:], ALU.mult))
                then(nc.vector.tensor_tensor(s, s, over_nodes(gain, NS), ALU.mult))
                if not first:
                    dve.wait_ge(x_in, 16)
                    then(nc.vector.tensor_tensor(s, s, over_nodes(bias, NS), ALU.add))
                    nc.vector.tensor_tensor(result[:], x_old[:], s, ALU.add).then_inc(result_done, 1)
                    return
                then(nc.vector.memset(result[:, :, NODE_U:NODE_S], 0.0))
                then(nc.vector.tensor_tensor(result[:, :, NODE_S:ROW], s, over_nodes(bias, NS), ALU.add))
                v = total[:, :, ROW_V:ROW_V + NV * XYZ]
                then(nc.vector.tensor_tensor(square[:, :, 0:NV * XYZ], v, v, ALU.mult))
                vsum = colsum[:, NV:NV + NV * XYZ]
                then(nc.vector.reduce_sum(vsum, square[:, :, 0:NV * XYZ].rearrange("p c k -> p k c"), AX_X))
                nc.vector.reduce_sum(colsum[:, 0:NV], vsum.rearrange("p (j c) -> p j c", c=XYZ),
                                     AX_X).then_inc(colsum_done, 1)
                dve.wait_ge(stat_done, 3)
                nc.vector.tensor_scalar(var[:, 0:NV], stat_ps[0:PN, 2 * NS:2 * NS + NV], 1.0 / (XYZ * N), EPS,
                                        ALU.mult, ALU.add).then_inc(var_done, 1)
                dve.wait_ge(std_done, 2)
                then(nc.vector.reciprocal(mean[:, 0:NV], std[:, 0:NV]))
                then(nc.vector.scalar_tensor_tensor(out=vgain[:], in0=vgain[:], scalar=float(1.0 / np.sqrt(3.0)),
                                                    in1=mean[:, 0:NV], op0=ALU.mult, op1=ALU.mult))
                then(nc.vector.tensor_copy(mean[:, 0:NV * XYZ].rearrange("p (j c) -> p j c", c=XYZ),
                                           vgain[:].unsqueeze(2).to_broadcast([PN, NV, XYZ])))
                then(nc.vector.tensor_tensor(result[:, :, NODE_V:NODE_V + NV * XYZ], v, over_nodes(mean, NV * XYZ),
                                             ALU.mult))
                split_in_three(nc, then, result[:], rest[:], [result3[:, :, h, :] for h in range(3)], result_done)


def gnn_kernel(nc, a, out):
    dram = {
        "norm_x": nc.dram_tensor("norm_x", [N, NS], F32),
        "norm_x3": nc.dram_tensor("norm_x3", [N, 3 * NS], BF16),
        "node3": nc.dram_tensor("node3", [N, 3 * ROW], BF16),
        "node": nc.dram_tensor("node", [N, ROW], F32),
        "place_rows": nc.dram_tensor("place_rows", [1, EP], BF16),
        "tile_min": nc.dram_tensor("tile_min_d", [ALL_TILES], F32),
        "tile_base": nc.dram_tensor("tile_base_d", [ALL_TILES], F32),
        "base": nc.dram_tensor("base_d", [STEPS], I32),
        "farthest": nc.dram_tensor("farthest_d", [SENDER_PARTS], F32),
        "recv_rows": nc.dram_tensor("recv_rows", [2, EP], BF16),
        "sum1": [nc.dram_tensor(f"sum1_{j}", [TABLE_ROWS, ROW], F32) for j in range(TABLES)],
        "sum2": [nc.dram_tensor(f"sum2_{j}", [TABLE_ROWS, COLS2], F32) for j in range(TABLES)],
    }
    with ExitStack() as ctx:
        def sb(name, shape, dt=F32):
            return ctx.enter_context(nc.sbuf_tensor(name, shape, dt))

        keep = {
            "unit": sb("unit", [P, ALL_TILES, XYZ]),
            "recv": sb("recv", [P, ALL_TILES]),
            "sender": sb("sender", [P, ALL_TILES], U32),
            "target": sb("target", [P, ALL_TILES], U32),
            "zero": sb("zero", [P, ZEROS]),
            "per_count": sb("per_count", [NODE_PARTS, NODE_COLS]),
            "by_part": sb("by_part", [P, 4]),
            "base": sb("base", [1, STEPS], I32),
            "in_windows": sb("in_windows", [1, 1], I32),
            "halves": sb("halves", [2, P], BF16),
        }
        for k in (1, 2):
            keep[f"w1_{k}"] = sb(f"w1_sb_{k}", [P, HID])
            keep[f"b1_{k}"] = sb(f"b1_sb_{k}", [P, 1])
            keep[f"w2_{k}"] = sb(f"w2_sb_{k}", [P, WN])
        constants(nc, keep)
        prepare(nc, a, dram, keep)
        edge_layer(nc, a, dram, keep, 1)
        node_layer(nc, a, dram, keep, 1, dram["node"][:, :])
        edge_layer(nc, a, dram, keep, 2)
        node_layer(nc, a, dram, keep, 2, out)


def _layout(x, src, dst, edge_attr_3, edge_attr_48, w):
    pad = EP - E
    attr = np.concatenate([edge_attr_48, np.zeros((pad, D), edge_attr_48.dtype)])
    vec = np.concatenate([edge_attr_3, np.zeros((pad, XYZ), edge_attr_3.dtype)])
    recv = np.concatenate([src, np.full(pad, PAD_NODE, src.dtype)])
    send = np.concatenate([dst, np.repeat(dst[-1:], pad)])
    cols = lambda v: np.ascontiguousarray(v.reshape(ALL_TILES, P).T)
    part = np.arange(P)
    weight = 3.0 ** (63 - part)
    arrays = {
        "x": x,
        "attr": np.ascontiguousarray(attr.reshape(STEPS, 2, HALF, D).transpose(1, 3, 0, 2)).reshape(2, D, STEPS * HALF),
        "vec": np.ascontiguousarray(vec.reshape(ALL_TILES, P, XYZ).transpose(1, 0, 2)),
        "recv_flat": recv.reshape(P, ALL_TILES),
        "recv_cols": cols(recv),
        "send_flat": send.reshape(SENDER_PARTS, ALL_TILES // SENDER_PARTS, P),
        "send_cols": cols(send),
        "by_part": np.stack([weight, 2 * weight, FIRST_SPARE + part, part], 1).astype(np.float32),
    }
    for k in (1, 2):
        f = f"L0_gnn_fc{k - 1}_"
        arrays[f"w1_{k}"] = w[f + "w1"]
        arrays[f"b1_{k}"] = w[f + "b1"].reshape(D, 1)
        for name, v in (("w2", w[f + "w2"]), ("b2", w[f + "b2"].reshape(1, WN))):
            wa = v[:, :NS * NS].reshape(-1, NS, NS)
            wb = v[:, NS * NS:].reshape((-1, NS, NV) if k == 1 else (-1, NV, NS))
            both = np.concatenate([wb, wa], axis=2 if k == 1 else 1)
            arrays[f"{name}_{k}"] = np.ascontiguousarray(both.reshape(-1, WN))
        arrays[f"gs_{k}"], arrays[f"bs_{k}"] = w[f"L0_gnn_bn{k - 1}_gs"], w[f"L0_gnn_bn{k - 1}_bs"]
    arrays["gv_1"] = w["L0_gnn_bn0_gv"]
    return arrays


def kernel(x, src, dst, edge_attr_3, edge_attr_48, **weights):
    import concourse.bacc as _bacc
    from concourse.bass_utils import run_bass_kernel_spmd as _run

    w = {name: np.asarray(v) for name, v in weights.items()}
    arrays = _layout(np.asarray(x), np.asarray(src), np.asarray(dst), np.asarray(edge_attr_3),
                     np.asarray(edge_attr_48), w)
    arrays = {f"in_{name}": np.ascontiguousarray(v) for name, v in arrays.items()}
    nc = _bacc.Bacc("TRN2", target_bir_lowering=False, num_devices=1)
    a = {name[3:]: nc.dram_tensor(name, v.shape, mybir.dt.from_np(v.dtype), kind="ExternalInput").ap()
         for name, v in arrays.items()}
    a["send_cols"] = a["send_cols"].bitcast(U32)
    out = nc.dram_tensor("out_0", [N, NS], F32, kind="ExternalOutput").ap()
    gnn_kernel(nc, a, out)
    r = _run(nc, [arrays], core_ids=[0])
    return r.results[0]["out_0"]
```
